# Optimizing a Trainium2 kernel written in Bass

```python
import numpy as np
import jax
import jax.numpy as jnp

def _softmax(x, axis=-1):
    return jax.nn.softmax(x, axis=axis)

def _gelu(x):
    return jax.nn.gelu(x, approximate=True)

def _silu(x):
    return jax.nn.silu(x)

def _sigmoid(x):
    return jax.nn.sigmoid(x)

def _layernorm(x, axis=-1, eps=1e-05):
    m = jnp.mean(x, axis=axis, keepdims=True)
    v = jnp.var(x, axis=axis, keepdims=True)
    return (x - m) / jnp.sqrt(v + eps)

def _scatter_add(tgt, idx, src, axis=0):
    return tgt.at[idx].add(src)

def _segment_sum(src, seg, n):
    return jax.ops.segment_sum(src, seg, n)
kernel_name = 'mk_adj_preln_d1_adj_r2_481446'

def setup_inputs(seed: int=0):
    np.random.seed(seed)
    _w = jnp.asarray

    def _rec_inputs():
        import jax
        import jax.numpy as jnp
        _gk = jax.random.key(seed)
        x = 7.22e-05 + 1 * jax.random.normal(jax.random.fold_in(_gk, 1), (64, 128, 1024), jnp.float32)
        _a = jax.random.bernoulli(jax.random.fold_in(_gk, 2), 0.125, (128, 128))
        _a = jnp.logical_or(_a, jnp.swapaxes(_a, -1, -2))
        _a = jnp.logical_or(_a, jnp.eye(128, dtype=bool))
        _af = _a.astype(jnp.float32)
        _af = _af * jax.random.uniform(jax.random.fold_in(_gk, 3), (128, 128), jnp.float32, 0.05, 0.27663)
        adj = _af
        return (x, adj)
    x, adj = _rec_inputs()

    def _L0_gnn_setup():
        import jax, jax.numpy as jnp
        import numpy as np
        N, B, T = (1024, 16, 128)
        key = jax.random.key(seed)
        k1, k2, k3, k4 = jax.random.split(key, 4)
        x = jax.random.normal(k1, (B, T, N), dtype=jnp.float32)
        weight = jax.random.normal(k2, (T, T), dtype=jnp.float32) * (1.0 / np.sqrt(T))
        bias = jax.random.normal(k3, (T,), dtype=jnp.float32) * 0.01
        u = jax.random.uniform(k4, (N * N, 2), dtype=jnp.float32, minval=1e-06, maxval=1.0 - 1e-06)
        gumbel = -jnp.log(-jnp.log(u))
        return {'x': x, 'weight': weight, 'bias': bias, 'gumbel': gumbel}
    _L0_gnn_all = _L0_gnn_setup()
    _L0_gnn_in = {k: v for k, v in _L0_gnn_all.items() if k in ('bias', 'gumbel')}
    del _L0_gnn_all
    return {'x': x, 'adj': adj, 'L0_gnn_bias': _L0_gnn_in['bias'], 'L0_gnn_gumbel': _L0_gnn_in['gumbel']}

def reference(x, adj, L0_gnn_bias, L0_gnn_gumbel):
    import jax
    import jax.numpy as jnp

    def _L0_gnn_ref(x, weight, bias, gumbel):
        import jax, jax.numpy as jnp
        import numpy as np
        N, B, T = (1024, 16, 128)
        xp = jnp.transpose(x, (2, 0, 1))
        n = xp.shape[0]
        xs = jax.lax.stop_gradient(xp)
        x_avg = xs.mean(axis=1)
        x_norm = x_avg / jnp.maximum(jnp.linalg.norm(x_avg, axis=-1, keepdims=True), 1e-12)
        sim = (x_norm @ x_norm.T + 1.0) * 0.5
        sim_flat = sim.reshape(-1)
        score0 = sim_flat + gumbel[:, 0]
        score1 = 1.0 - sim_flat + gumbel[:, 1]
        adj = (score0 > score1).astype(xp.dtype).reshape(n, n)
        adj_sym = jnp.clip(adj + adj.T, 0.0, 1.0)
        nmask = jnp.clip(adj_sym + jnp.eye(n, dtype=xp.dtype), 0.0, 1.0)
        common = nmask @ nmask.T
        max_common = common.max()
        valid = adj_sym * (common > 1.0).astype(xp.dtype) > 0
        struct = jnp.where(valid, common / max_common * common, 0.0)
        W = adj * struct
        deg = W.sum(axis=0)
        dinv = jnp.where(deg > 0, deg ** (-0.5), 0.0)
        Wn = dinv[:, None] * W * dinv[None, :]
        xw = jnp.einsum('nbt,to->nbo', xp, weight)
        out = jnp.einsum('sd,sbt->dbt', Wn, xw) + bias
        return jnp.transpose(out, (1, 2, 0))
    h = jnp.maximum(_layernorm(x, axis=-1), 0.0)
    x = x + _L0_gnn_ref(h, adj, L0_gnn_bias, L0_gnn_gumbel)
    return x

_drawn_inputs = setup_inputs


def setup_inputs(seed=0):
    import zlib

    import numpy as np

    out = dict(_drawn_inputs(seed))
    spreads = {}
    factors = {'L0_gnn_bias': 8.0, 'L0_gnn_gumbel': 3.781}
    for name, (base, spread) in spreads.items():
        noise = np.random.default_rng([zlib.crc32(name.encode()), seed]).standard_normal(out[name].shape)
        drawn = base * np.exp(spread * noise) if base else spread * noise
        out[name] = jnp.asarray(drawn.astype(out[name].dtype))
    for name, factor in factors.items():
        out[name] = (out[name] * factor).astype(out[name].dtype)
    return out
```

```python
from contextlib import ExitStack

import concourse.bass as bass
from concourse import mybir

ALU = mybir.AluOpType
ACT = mybir.ActivationFunctionType
F32 = mybir.dt.float32
F32R = mybir.dt.float32r
BF16 = mybir.dt.bfloat16
F16 = mybir.dt.float16
AX_X = mybir.AxisListType.X
RMAX = bass.bass_isa.ReduceOp.max
ds = bass.ds

EPS = 1e-5
NORM_MIN = 1e-12
DEG_MIN = 1e-6


def gnn_program(nc, x, weight, bias, gumbel, out):
    B, T, N = x.shape
    P = 128
    S = N // P
    H = N // 2
    G = 4
    RING = 4
    STEPS = B // G // RING
    CHUNKS_STEP = S // STEPS
    XB = 4
    assert T == P and B % (G * RING) == 0 and S % STEPS == 0 and CHUNKS_STEP == 2 and B % XB == 0

    x_btn = x.rearrange("b t n -> t b n")
    out_btn = out.rearrange("b t n -> t b n")
    gumbel_rows = gumbel.rearrange("(c p n) k -> p c n k", p=P, n=N)
    bias_col = bias.rearrange("(t a) -> t a", a=1)

    with ExitStack() as ctx:
        top = [16512]

        def place(offset, name, shape, dtype):
            return nc.alloc_sbuf_tensor_at(name, shape, dtype, offset=offset)

        def region(size):
            start = top[0]
            top[0] += size
            return start

        def keep(name, shape, dtype=F32):
            size = 1
            for s in shape[1:]:
                size *= s
            return place(region(-(-size * (2 if dtype in (BF16, F16) else 4) // 32) * 32), name, shape, dtype)

        def sem(name):
            return ctx.enter_context(nc.semaphore(name))

        ROW = 4 * N

        ident = keep("ident", [P, P])
        ident_bf = keep("ident_bf", [P, P], BF16)
        ones = keep("ones", [P, P])
        ones_r = keep("ones_r", [P, 2], F32R)
        zeros = keep("zeros", [P, H])
        w_in = keep("w_in", [P, P])
        w_hi = keep("w_hi", [P, P], F32R)
        w_lo = keep("w_lo", [P, P], F32R)
        bias_sb = keep("bias_sb", [P, 1])
        halves = keep("halves", [P, G, 2, 6])
        mean_var = keep("mean_var", [P, G, 2])
        var_eps = keep("var_eps", [P, G])
        waiting = keep("waiting", [P, 1])
        stdev = keep("stdev", [P, G])
        inv0 = keep("inv0", [P, G])
        newton_a = keep("newton_a", [P, G])
        newton_b = keep("newton_b", [P, G])
        newton_c = keep("newton_c", [P, G])
        rstd = keep("rstd", [P, B])
        shift = keep("shift", [P, B])
        col_v = keep("col_v", [P, S])
        col_sqrt = keep("col_sqrt", [P, S])
        col_inv = keep("col_inv", [P, S])
        col_a = keep("col_a", [P, S])
        col_b = keep("col_b", [P, S])
        col_c = keep("col_c", [P, S])
        inv_norm = keep("inv_norm", [P, S])
        degree = keep("degree", [P, S])
        has_edge = keep("has_edge", [P, S])
        dinv = keep("dinv", [P, S])
        dinv_out = keep("dinv_out", [P, S])
        self_common = keep("self_common", [P, S])
        all_common = keep("all_common", [P, S])
        max_common = keep("max_common", [P, 1])
        inv_max = keep("inv_max", [P, 1])

        a = region(RING * G * ROW)
        x1 = place(a, "x1", [P, RING, G, N], F32)
        W_hi = place(a, "W_hi", [P, S, N], F32R)
        W_lo = place(a + S * ROW, "W_lo", [P, S, N], F32R)
        b_ = region(S * ROW)
        noise = place(b_, "noise", [P, S, N], F32)
        y = place(b_, "y", [P, N], F32)
        y_hi = place(b_ + ROW, "y_hi", [P, 2, N], F32R)
        y_lo = place(b_ + 3 * ROW, "y_lo", [P, 2, N], F32R)
        scaled = place(b_ + 5 * ROW, "scaled", [P, 2, N], F32)
        c_ = region(4 * ROW)
        pairs = place(c_, "pairs", [P, 2, N, 2], F32)
        square = place(c_, "square", [P, 2, N], F32)
        edges_common = place(c_ + 2 * ROW, "edges_common", [P, 2, N], F16)
        adj = place(region(S * N * 2), "adj", [P, S, N], BF16)
        nmask = place(region(S * N * 2), "nmask", [P, S, N], BF16)
        x2 = place(region(XB * ROW), "x2", [P, XB, N], F32)
        h = place(region(ROW), "h", [P, N], F32)
        h_hi = place(region(ROW), "h_hi", [P, N], F32R)
        h_lo = place(region(ROW), "h_lo", [P, N], F32R)
        g_ = region(4 * ROW)
        avg = place(g_, "avg", [P, N], F32)
        avg_sq = place(g_ + ROW, "avg_sq", [P, N], F32)
        feats = place(g_ + 2 * ROW, "feats", [P, N], F32)
        result = place(g_, "result", [P, 2, N], F32)
        dinv_row = place(g_ + 2 * ROW, "dinv_row", [P, N], F32)
        diag = place(g_ + 3 * ROW, "diag", [P, S, P], F32)
        assert top[0] <= nc.sbuf_usable_end

        ps = ctx.enter_context(nc.psum_tensor("ps", [P, 4, N], F32))
        SUM, COLS, ROWS, Y = 0, 1, 2, 3

        consts_ready = sem("consts_ready")
        consts_zero = sem("consts_zero")
        params_in = sem("params_in")
        w_hi_ready = sem("w_hi_ready")
        w_lo_ready = sem("w_lo_ready")
        ones_r_ready = sem("ones_r_ready")
        x1_in = [sem(f"x1_in{k}") for k in range(RING)]
        pairs_in = [sem(f"pairs_in{k}") for k in range(2)]
        noise_made = sem("noise_made")
        halves_ready = sem("halves_ready")
        mean_var_ready = sem("mean_var_ready")
        var_eps_ready = sem("var_eps_ready")
        stdev_ready = sem("stdev_ready")
        newton_step = sem("newton_step")
        norm_ready = sem("norm_ready")
        h1_ready = sem("h1_ready")
        h1_summed = sem("h1_summed")
        sum_done = sem("sum_done")
        avg_ready = sem("avg_ready")
        avg_sq_ready = sem("avg_sq_ready")
        sumsq_done = sem("sumsq_done")
        col_v_ready = sem("col_v_ready")
        col_sqrt_ready = sem("col_sqrt_ready")
        col_step = sem("col_step")
        diag_ready = sem("diag_ready")
        row_done = sem("row_done")
        feats_ready = sem("feats_ready")
        sim_done = sem("sim_done")
        adj_ready = sem("adj_ready")
        sym_done = sem("sym_done")
        nmask_act = sem("nmask_act")
        nmask_dve = sem("nmask_dve")
        common_done = sem("common_done")
        self_ready = sem("self_ready")
        edges_all = sem("edges_all")
        edges_ready = sem("edges_ready")
        square_ready = sem("square_ready")
        W_hi_ready = sem("W_hi_ready")
        W_lo_ready = sem("W_lo_ready")
        deg_done = sem("deg_done")
        max_ready = sem("max_ready")
        dinv_ready = sem("dinv_ready")
        dinv_row_ready = sem("dinv_row_ready")
        x2_in = [sem(f"x2_in{k}") for k in range(XB)]
        h_ready = sem("h_ready")
        h_hi_ready = sem("h_hi_ready")
        h_lo_ready = sem("h_lo_ready")
        y_done = sem("y_done")
        y_ready = sem("y_ready")
        y_hi_ready = sem("y_hi_ready")
        y_lo_ready = sem("y_lo_ready")
        agg_done = sem("agg_done")
        scaled_ready = sem("scaled_ready")
        result_ready = sem("result_ready")
        result_stored = [sem(f"result_stored{k}") for k in range(2)]

        def rows(t):
            return t.rearrange("p (c n) -> p c n", n=P)

        block = ctx.enter_context(nc.Block())

        @block.sync
        def _(sp):
            def load_group(j, k):
                sp.dma_start(x1[:, k], x_btn[:, ds((j * RING + k) * G, G), :]).then_inc(x1_in[k], 16)

            def load_pairs(j, k):
                sp.dma_start(pairs[:, k], gumbel_rows[:, j * 2 + k]).then_inc(pairs_in[k], 16)

            for k in range(RING):
                load_group(0, k)
                if k == 0:
                    sp.dma_start(w_in[:], weight).then_inc(params_in, 16)
                    sp.dma_start(bias_sb[:], bias_col).then_inc(params_in, 16)
                if k % 2:
                    load_pairs(0, k // 2)
            with sp.Fori(1, STEPS) as j:
                for k in range(RING):
                    sp.wait_ge(h1_summed, (j - 1) * RING + k + 1)
                    load_group(j, k)
                    if k % 2:
                        sp.wait_ge(noise_made, (j - 1) * 2 + k // 2 + 1)
                        load_pairs(j, k // 2)
            for k in range(XB):
                sp.dma_start(x2[:, k], x_btn[:, k]).then_inc(x2_in[k], 16)

            def store(b, parity):
                sp.wait_ge(result_ready, b + 1)
                sp.dma_start(out_btn[:, ds(b, 1), :], result[:, parity:parity + 1]).then_inc(result_stored[parity], 16)

            with sp.Fori(0, B // XB - 1) as i:
                b = i * XB
                for k in range(XB):
                    store(b + k, k % 2)
                    sp.dma_start(x2[:, k:k + 1], x_btn[:, ds(b + k + XB, 1), :]).then_inc(x2_in[k], 16)
            for k in range(XB):
                store(B - XB + k, k % 2)
            for k in range(2):
                sp.wait_ge(result_stored[k], 16 * (B // 2 + 1))

        @block.gpsimd
        def _(pool):
            pool.memset(ident[:], 0.0).then_inc(consts_zero, 1)
            pool.memset(ones[:], 1.0).then_inc(consts_ready, 1)
            pool.memset(zeros[:], 0.0).then_inc(consts_ready, 1)
            pool.wait_ge(consts_zero, 1)
            pool.affine_select(out=ident[:], in_=ident[:], compare_op=ALU.not_equal, fill=1.0, base=0,
                               pattern=[[-1, P]], channel_multiplier=1).then_inc(consts_ready, 1)
            pool.wait_ge(consts_ready, 3)
            pool.tensor_copy(ident_bf[:], ident[:]).then_inc(consts_ready, 1)
            pool.wait_ge(params_in, 32)
            pool.wait_ge(w_hi_ready, 1)
            pool.tensor_tensor(w_lo[:], w_in[:], w_hi[:].bitcast(F32), ALU.subtract).then_inc(w_lo_ready, 1)

            with pool.Fori(0, STEPS) as j:
                for k in range(2):
                    pool.wait_ge(pairs_in[k], 16 * (j + 1))
                    pool.tensor_tensor(noise[:, ds(j * 2 + k, 1), :], pairs[:, k:k + 1, :, 1], pairs[:, k:k + 1, :, 0],
                                       ALU.subtract).then_inc(noise_made, 1)

            def low_h(b):
                pool.wait_ge(h_hi_ready, b + 1)
                if not (isinstance(b, int) and b == 0):
                    pool.wait_ge(y_done, b)
                pool.tensor_tensor(h_lo[:], h[:], h_hi[:].bitcast(F32), ALU.subtract).then_inc(h_lo_ready, 1)

            def low_y(b, parity):
                pool.wait_ge(y_hi_ready, b + 1)
                if not (isinstance(b, int) and b < 2):
                    pool.wait_ge(agg_done, b - 1)
                pool.tensor_tensor(y_lo[:, parity], y[:], y_hi[:, parity].bitcast(F32),
                                   ALU.subtract).then_inc(y_lo_ready, 1)

            for s in range(S):
                pool.wait_ge(W_hi_ready, s + 1)
                pool.tensor_tensor(W_lo[:, s], square[:, s % 2], W_hi[:, s].bitcast(F32),
                                   ALU.subtract).then_inc(W_lo_ready, 1)
            pool.wait_ge(self_ready, S)
            pool.partition_all_reduce(all_common[:], self_common[:], P, RMAX).then_inc(max_ready, 1)
            low_h(0)
            for b in range(3):
                low_h(b + 1)
                low_y(b, b % 2)
            with pool.Fori(0, B // XB - 1) as i:
                b = i * XB + 3
                for k in range(XB):
                    low_h(b + k + 1)
                    low_y(b + k, (3 + k) % 2)
            low_y(B - 1, (B - 1) % 2)

        @block.scalar
        def _(act):
            act.wait_ge(params_in, 32)
            act.copy(w_hi[:], w_in[:]).then_inc(w_hi_ready, 1)
            act.wait_ge(consts_ready, 1)
            act.copy(ones_r[:], ones[:, 0:2]).then_inc(ones_r_ready, 1)

            with act.Fori(0, STEPS) as j:
                for k in range(RING):
                    g = j * RING + k
                    act.wait_ge(var_eps_ready, g + 1)
                    act.activation(stdev[:], var_eps[:], ACT.Sqrt).then_inc(stdev_ready, 1)
                    act.wait_ge(norm_ready, g + 1)
                    for q in range(G):
                        act.activation(x1[:, k, q], x1[:, k, q], ACT.Relu, scale=rstd[:, ds(g * G + q, 1)],
                                       bias=shift[:, ds(g * G + q, 1)]).then_inc(h1_ready, 1)

            act.wait_ge(sum_done, 1)
            act.activation(avg_sq[:], ps[:, SUM], ACT.Square, scale=1.0 / B).then_inc(avg_sq_ready, 1)
            act.activation(avg[:], ps[:, SUM], ACT.Copy, scale=1.0 / B).then_inc(avg_ready, 1)
            act.wait_ge(col_v_ready, 1)
            act.activation(col_sqrt[:], col_v[:], ACT.Sqrt).then_inc(col_sqrt_ready, 1)

            for s in range(S):
                act.wait_ge(sym_done, s + 1)
                act.activation(nmask[:, s, 0:H], ps[:, 2 + s % 2, 0:H], ACT.Sign).then_inc(nmask_act, 1)

            for s in range(S):
                act.wait_ge(edges_ready, s + 1)
                if s >= 2:
                    act.wait_ge(W_lo_ready, s - 1)
                act.activation(square[:, s % 2], edges_common[:, s % 2], ACT.Square).then_inc(square_ready, 1)
                act.wait_ge(square_ready, s + 1)
                act.copy(W_hi[:, s], square[:, s % 2]).then_inc(W_hi_ready, 1)

            def high_h(b, slot, turn):
                act.wait_ge(x2_in[slot], 16 * (turn + 1))
                if not (isinstance(b, int) and b == 0):
                    act.wait_ge(h_lo_ready, b)
                act.activation(h[:], x2[:, slot], ACT.Relu, scale=rstd[:, ds(b, 1)],
                               bias=shift[:, ds(b, 1)]).then_inc(h_ready, 1)
                act.wait_ge(h_ready, b + 1)
                if not (isinstance(b, int) and b == 0):
                    act.wait_ge(y_done, b)
                act.copy(h_hi[:], h[:]).then_inc(h_hi_ready, 1)

            def high_y(b, parity):
                act.wait_ge(y_ready, b + 1)
                if not (isinstance(b, int) and b < 2):
                    act.wait_ge(agg_done, b - 1)
                act.copy(y_hi[:, parity], y[:]).then_inc(y_hi_ready, 1)

            high_h(0, 0, 0)
            act.wait_ge(col_v_ready, 2)
            act.activation(col_sqrt[:], col_v[:], ACT.Sqrt).then_inc(col_sqrt_ready, 1)
            act.wait_ge(row_done, 2)
            act.copy(dinv_row[:], ps[:, ROWS]).then_inc(dinv_row_ready, 1)
            for b in range(3):
                high_h(b + 1, b + 1, 0)
                high_y(b, b % 2)
            with act.Fori(1, B // XB) as i:
                for k in range(XB):
                    b = i * XB + k
                    high_h(b, k, i)
                    high_y(b - 1, (k + 1) % 2)
            high_y(B - 1, (B - 1) % 2)

        @block.vector
        def _(dve):
            def refine(v, root, inv, tmp, out_, sem_, n0):
                dve.reciprocal(inv, root).then_inc(sem_, 1)
                dve.wait_ge(sem_, n0 + 1)
                dve.tensor_tensor(tmp[0], inv, inv, ALU.mult).then_inc(sem_, 1)
                dve.wait_ge(sem_, n0 + 2)
                dve.tensor_tensor(tmp[1], tmp[0], v, ALU.mult).then_inc(sem_, 1)
                dve.wait_ge(sem_, n0 + 3)
                dve.tensor_scalar(tmp[2], tmp[1], -0.5, 1.5, ALU.mult, ALU.add).then_inc(sem_, 1)
                dve.wait_ge(sem_, n0 + 4)
                dve.tensor_tensor(out_, tmp[2], inv, ALU.mult).then_inc(sem_, 1)
                dve.wait_ge(sem_, n0 + 5)

            with dve.Fori(0, STEPS) as j:
                for k in range(RING):
                    g = j * RING + k
                    dve.wait_ge(x1_in[k], 16 * (j + 1))
                    for q in range(G):
                        for half in range(2):
                            dve.bn_stats(halves[:, q, half], x1[:, k, q, half * H:half * H + H]).then_inc(halves_ready, 1)
                    dve.wait_ge(halves_ready, (g + 1) * 2 * G)
                    dve.memset(waiting[:], 0.0)
                    for q in range(G):
                        dve.bn_aggr(mean_var[:, q], halves[:, q]).then_inc(mean_var_ready, 1)
                    dve.wait_ge(mean_var_ready, (g + 1) * G)
                    dve.tensor_scalar(var_eps[:], mean_var[:, :, 1], EPS, None, ALU.add).then_inc(var_eps_ready, 1)
                    dve.wait_ge(stdev_ready, g + 1)
                    refine(var_eps[:], stdev[:], inv0[:], (newton_a[:], newton_b[:], newton_c[:]),
                           rstd[:, ds(g * G, G)], newton_step, g * 5)
                    dve.scalar_tensor_tensor(out=shift[:, ds(g * G, G)], in0=mean_var[:, :, 0], scalar=-1.0,
                                             in1=rstd[:, ds(g * G, G)], op0=ALU.mult, op1=ALU.mult).then_inc(norm_ready, 1)

            dve.wait_ge(sumsq_done, 1)
            dve.tensor_scalar(col_v[:], ps[:, COLS, 0:S], NORM_MIN ** 2, None, ALU.max).then_inc(col_v_ready, 1)
            dve.wait_ge(col_sqrt_ready, 1)
            cols = (col_a[:], col_b[:], col_c[:])
            refine(col_v[:], col_sqrt[:], col_inv[:], cols, inv_norm[:], col_step, 0)
            ident_rows = ident[:].unsqueeze(1).to_broadcast([P, S, P])
            dve.wait_ge(consts_ready, 4)
            dve.tensor_tensor(diag[:], ident_rows, inv_norm[:].unsqueeze(2).to_broadcast([P, S, P]),
                              ALU.mult).then_inc(diag_ready, 1)
            dve.wait_ge(row_done, 1)
            dve.wait_ge(avg_ready, 1)
            dve.tensor_tensor(feats[:], avg[:], ps[:, ROWS], ALU.mult).then_inc(feats_ready, 1)

            dve.wait_ge(noise_made, S)
            for s in range(S):
                dve.wait_ge(sim_done, s + 1)
                dve.tensor_tensor(adj[:, s], ps[:, s % 2], noise[:, s], ALU.is_gt).then_inc(adj_ready, 1)
            for s in range(S):
                dve.wait_ge(sym_done, s + 1)
                dve.tensor_scalar(nmask[:, s, H:N], ps[:, 2 + s % 2, H:N], 1.0, None, ALU.min).then_inc(nmask_dve, 1)
            for s in range(S):
                node = slice(s * P, s * P + P)
                dve.wait_ge(common_done, s + 1)
                if s >= 2:
                    dve.wait_ge(square_ready, s - 1)
                dve.tensor_tensor(edges_common[:, s % 2], ps[:, s % 2], adj[:, s], ALU.mult).then_inc(edges_all, 1)
                dve.tensor_reduce(self_common[:, s:s + 1], ps[:, s % 2, node], AX_X, ALU.max).then_inc(self_ready, 1)
                dve.wait_ge(edges_all, s + 1)
                dve.scalar_tensor_tensor(out=edges_common[:, s % 2, node], in0=ps[:, s % 2, node], scalar=1.0,
                                         in1=edges_common[:, s % 2, node], op0=ALU.is_gt,
                                         op1=ALU.mult).then_inc(edges_ready, 1)

            dve.wait_ge(max_ready, 1)
            dve.tensor_reduce(max_common[:], all_common[:], AX_X, ALU.max).then_inc(col_step, 1)
            dve.wait_ge(col_step, 6)
            dve.reciprocal(inv_max[:], max_common[:]).then_inc(col_step, 1)
            dve.wait_ge(col_step, 7)
            dve.wait_ge(deg_done, 1)
            dve.tensor_scalar(degree[:], ps[:, COLS, 0:2 * S:2], inv_max[:, 0:1], None, ALU.mult).then_inc(col_step, 1)
            dve.wait_ge(col_step, 8)
            dve.tensor_scalar(col_v[:], degree[:], DEG_MIN, None, ALU.max).then_inc(col_v_ready, 1)
            dve.tensor_scalar(has_edge[:], degree[:], 0.0, None, ALU.is_gt).then_inc(col_step, 1)
            dve.wait_ge(col_sqrt_ready, 2)
            refine(col_v[:], col_sqrt[:], col_inv[:], cols, inv_norm[:], col_step, 9)
            dve.tensor_tensor(dinv[:], inv_norm[:], has_edge[:], ALU.mult).then_inc(dinv_ready, 1)
            dve.wait_ge(dinv_ready, 1)
            dve.tensor_scalar(dinv_out[:], dinv[:], inv_max[:, 0:1], None, ALU.mult).then_inc(dinv_ready, 1)
            dve.wait_ge(dinv_ready, 2)
            dve.tensor_tensor(diag[:], ident_rows, dinv_out[:].unsqueeze(2).to_broadcast([P, S, P]),
                              ALU.mult).then_inc(diag_ready, 1)

            dinv_rows = dinv[:].unsqueeze(2).to_broadcast([P, S, P])

            def scale_y(b):
                dve.wait_ge(y_done, b + 1)
                if not (isinstance(b, int) and b == 0):
                    dve.wait_ge(y_hi_ready, b)
                    dve.wait_ge(y_lo_ready, b)
                dve.tensor_tensor(rows(y[:]), rows(ps[:, Y]), dinv_rows, ALU.mult).then_inc(y_ready, 1)

            def finish(b, parity, slot, stored):
                dve.wait_ge(agg_done, b + 1)
                dve.tensor_tensor(scaled[:, parity], ps[:, parity], dinv_row[:], ALU.mult).then_inc(scaled_ready, 1)
                dve.wait_ge(scaled_ready, b + 1)
                dve.wait_ge(result_stored[parity], stored)
                dve.scalar_tensor_tensor(out=result[:, parity], in0=scaled[:, parity], scalar=bias_sb[:, 0:1],
                                         in1=x2[:, slot], op0=ALU.add, op1=ALU.add).then_inc(result_ready, 1)

            dve.nop().then_inc(result_stored[0], 16)
            dve.nop().then_inc(result_stored[1], 16)
            scale_y(0)
            dve.wait_ge(dinv_row_ready, 1)
            for b in range(3):
                scale_y(b + 1)
                finish(b, b % 2, b, 16 * (b // 2 + 1))
            with dve.Fori(1, B // XB) as i:
                for k in range(XB):
                    b = i * XB + k
                    scale_y(b)
                    finish(b - 1, (k + 1) % 2, (k - 1) % XB, 16 * (i * 2 + (k - 1) // 2 + 1))
            finish(B - 1, (B - 1) % 2, XB - 1, 16 * ((B - 1) // 2 + 1))

        @block.tensor
        def _(pe):
            pe.wait_ge(consts_ready, 4)
            for half in range(2):
                pe.matmul(ps[:, SUM, half * H:half * H + H], ident[:], zeros[:], start=True, stop=False)
            with pe.Fori(0, STEPS) as j:
                for k in range(RING):
                    for q in range(G):
                        pe.wait_ge(h1_ready, (j * RING + k) * G + q + 1)
                        for half in range(2):
                            mm = pe.matmul(ps[:, SUM, half * H:half * H + H], ident[:],
                                           x1[:, k, q, half * H:half * H + H], start=False, stop=False)
                    mm.then_inc(h1_summed, 1)
            for half in range(2):
                mm = pe.matmul(ps[:, SUM, half * H:half * H + H], ident[:], zeros[:], start=False, stop=True)
            mm.then_inc(sum_done, 1)

            pe.wait_ge(avg_sq_ready, 1)
            for s in range(S):
                mm = pe.matmul(ps[:, COLS, s:s + 1], avg_sq[:, s * P:s * P + P], ones[:, 0:1], start=True, stop=True)
            mm.then_inc(sumsq_done, 1)

            def spread_diag(n):
                pe.wait_ge(diag_ready, n)
                for half in range(2):
                    mm = pe.matmul(ps[:, ROWS, half * H:half * H + H], ones[:],
                                   diag[:, half * (S // 2):(half + 1) * (S // 2), :], start=True, stop=True)
                mm.then_inc(row_done, 1)

            spread_diag(1)
            pe.wait_ge(feats_ready, 1)
            for s in range(S):
                if s >= 2:
                    pe.wait_ge(adj_ready, s - 1)
                for half in range(2):
                    mm = pe.matmul(ps[:, s % 2, half * H:half * H + H], feats[:, s * P:s * P + P],
                                   feats[:, half * H:half * H + H], start=True, stop=True)
                mm.then_inc(sim_done, 1)
            pe.wait_ge(adj_ready, S)
            for s in range(S):
                if s >= 2:
                    pe.wait_ge(nmask_act, s - 1)
                    pe.wait_ge(nmask_dve, s - 1)
                for half in range(2):
                    bank = ps[:, 2 + s % 2, half * H:half * H + H]
                    mine = range(half * (S // 2), (half + 1) * (S // 2))
                    for d in mine:
                        block_d = bank[:, (d - mine[0]) * P:(d - mine[0] + 1) * P]
                        pe.matmul(block_d, adj[:, d, s * P:s * P + P], ident_bf[:], start=(d == mine[0]), stop=False)
                        if d == s:
                            pe.matmul(block_d, ident_bf[:], ident_bf[:], start=False, stop=False)
                    mm = pe.matmul(bank, ident_bf[:], adj[:, s, half * H:half * H + H], start=False, stop=True)
                mm.then_inc(sym_done, 1)
            pe.wait_ge(nmask_act, S)
            pe.wait_ge(nmask_dve, S)
            for s in range(S):
                if s >= 2:
                    pe.wait_ge(edges_ready, s - 1)
                    pe.wait_ge(self_ready, s - 1)
                for c in range(S):
                    for half in range(2):
                        mm = pe.matmul(ps[:, s % 2, half * H:half * H + H], nmask[:, c, s * P:s * P + P],
                                       nmask[:, c, half * H:half * H + H], start=(c == 0), stop=(c == S - 1))
                mm.then_inc(common_done, 1)

            def project(b):
                pe.wait_ge(h_hi_ready, b + 1)
                pe.wait_ge(h_lo_ready, b + 1)
                if not (isinstance(b, int) and b == 0):
                    pe.wait_ge(y_ready, b)
                for s in range(S):
                    node = slice(s * P, s * P + P)
                    pe.matmul(ps[:, Y, node], h_hi[:, node], w_hi[:], start=True, stop=False)
                    pe.matmul(ps[:, Y, node], h_hi[:, node], w_lo[:], start=False, stop=False)
                    mm = pe.matmul(ps[:, Y, node], h_lo[:, node], w_hi[:], start=False, stop=True)
                mm.then_inc(y_done, 1)

            def aggregate(b, parity):
                pe.wait_ge(y_hi_ready, b + 1)
                pe.wait_ge(y_lo_ready, b + 1)
                if not (isinstance(b, int) and b < 2):
                    pe.wait_ge(scaled_ready, b - 1)
                for s in range(S):
                    node = slice(s * P, s * P + P)
                    for y_part, W_part in ((y_hi, W_hi), (y_hi, W_lo), (y_lo, W_hi)):
                        for half in range(2):
                            mm = pe.matmul(ps[:, parity, half * H:half * H + H], y_part[:, parity, node],
                                           W_part[:, s, half * H:half * H + H],
                                           start=(s == 0 and y_part is y_hi and W_part is W_hi),
                                           stop=(s == S - 1 and y_part is y_lo))
                mm.then_inc(agg_done, 1)

            pe.wait_ge(w_lo_ready, 1)
            project(0)
            pe.wait_ge(W_hi_ready, S)
            pe.wait_ge(W_lo_ready, S)
            pe.wait_ge(ones_r_ready, 1)
            for s in range(S):
                for c in range(S):
                    for part in (W_hi, W_lo):
                        mm = pe.matmul(ps[:, COLS, 2 * s:2 * s + 2], part[:, c, s * P:s * P + P], ones_r[:],
                                       start=(c == 0 and part is W_hi), stop=(c == S - 1 and part is W_lo))
            mm.then_inc(deg_done, 1)
            spread_diag(2)
            project(1)
            pe.wait_ge(edges_ready, S)
            aggregate(0, 0)
            with pe.Fori(0, (B - 2) // 2) as i:
                b = i * 2 + 1
                for k in range(2):
                    project(b + k + 1)
                    aggregate(b + k, (1 + k) % 2)
            aggregate(B - 1, (B - 1) % 2)


_INS = ['x', 'adj', 'L0_gnn_bias', 'L0_gnn_gumbel']
_OUTS = [((64, 128, 1024), 'float32')]


def kernel(**inputs):
    import numpy as _np
    import concourse.bacc as _bacc
    from concourse import mybir as _mybir
    from concourse.bass_utils import run_bass_kernel_spmd as _run

    nc = _bacc.Bacc("TRN2", target_bir_lowering=False, num_devices=1)
    arrays, args = {}, []
    for name in _INS:
        a = _np.ascontiguousarray(inputs[name])
        arrays[f"in_{name}_dram"] = a
        args.append(nc.dram_tensor(f"in_{name}_dram", a.shape, _mybir.dt.from_np(a.dtype), kind="ExternalInput").ap())
    for i, (shape, dtype) in enumerate(_OUTS):
        dt = _mybir.dt.from_np(_np.dtype(dtype))
        args.append(nc.dram_tensor(f"out_{i}_dram", shape, dt, kind="ExternalOutput").ap())
    gnn_program(nc, *args)
    r = _run(nc, [arrays], core_ids=[0])
    got = tuple(r.results[0][f"out_{i}_dram"] for i in range(len(_OUTS)))
    return got[0]
```

```python
from contextlib import ExitStack

import concourse.bass as bass
from concourse import mybir

ALU = mybir.AluOpType
ACT = mybir.ActivationFunctionType
F32 = mybir.dt.float32
F32R = mybir.dt.float32r
BF16 = mybir.dt.bfloat16
F16 = mybir.dt.float16
I32 = mybir.dt.int32
AX_X = mybir.AxisListType.X
RMAX = bass.bass_isa.ReduceOp.max
ds = bass.ds

EPS = 1e-5
NORM_MIN = 1e-12
DEG_MIN = 1e-6
H_SCALE = 1024.0
W_TOP = 2.0 ** 14
W_MIN = 1e-30
EXPONENT = 0x7F800000


def gnn_program(nc, x, weight, bias, gumbel, out):
    B, T, N = x.shape
    P = 128
    S = N // P
    H = N // 2
    G = 4
    RING = 4
    STEPS = B // G // RING
    CHUNKS_STEP = S // STEPS
    XB = 4
    assert T == P and B % (G * RING) == 0 and S % STEPS == 0 and CHUNKS_STEP == 2 and B % XB == 0

    x_btn = x.rearrange("b t n -> t b n")
    out_btn = out.rearrange("b t n -> t b n")
    gumbel_rows = gumbel.rearrange("(c p n) k -> p c n k", p=P, n=N)
    bias_col = bias.rearrange("(t a) -> t a", a=1)

    with ExitStack() as ctx:
        top = [16512]

        def place(offset, name, shape, dtype):
            return nc.alloc_sbuf_tensor_at(name, shape, dtype, offset=offset)

        def region(size):
            start = top[0]
            top[0] += size
            return start

        def keep(name, shape, dtype=F32):
            size = 1
            for s in shape[1:]:
                size *= s
            return place(region(-(-size * (2 if dtype in (BF16, F16) else 4) // 32) * 32), name, shape, dtype)

        def sem(name):
            return ctx.enter_context(nc.semaphore(name))

        ROW = 4 * N

        ident = keep("ident", [P, P])
        ident_bf = keep("ident_bf", [P, P], BF16)
        ones = keep("ones", [P, P])
        zeros = keep("zeros", [P, H])
        w_in = keep("w_in", [P, P])
        w_cols = keep("w_cols", [P, P])
        w_hi = keep("w_hi", [P, P], F16)
        w_lo = keep("w_lo", [P, P], F16)
        w_max = keep("w_max", [P, 1])
        w_pow = keep("w_pow", [P, 1])
        w_pow_inv = keep("w_pow_inv", [P, 1])
        unscale = keep("unscale", [P, 1])
        bias_sb = keep("bias_sb", [P, 1])
        halves = keep("halves", [P, 2, G, 2, 6])
        mean_var = keep("mean_var", [P, 2, G, 2])
        waiting = keep("waiting", [P, 1])
        c_eps, c_neg, c_half, c_three = (keep(f"c_{n}", [P, G]) for n in ("eps", "neg", "half", "three"))
        var_eps = keep("var_eps", [P, G])
        var_half = keep("var_half", [P, G])
        neg_mean = keep("neg_mean", [P, G])
        stdev = keep("stdev", [P, G])
        inv0 = keep("inv0", [P, G])
        newton_a = keep("newton_a", [P, G])
        newton_b = keep("newton_b", [P, G])
        newton_c = keep("newton_c", [P, G])
        affine = keep("affine", [P, 2, 2, G])
        norms = keep("norms", [P, B // G, 2, G])
        col_v = keep("col_v", [P, S])
        col_sqrt = keep("col_sqrt", [P, S])
        col_inv = keep("col_inv", [P, S])
        col_a = keep("col_a", [P, S])
        col_b = keep("col_b", [P, S])
        col_c = keep("col_c", [P, S])
        inv_norm = keep("inv_norm", [P, S])
        degree = keep("degree", [P, S])
        degree_n = keep("degree_n", [P, S])
        has_edge = keep("has_edge", [P, S])
        dinv = keep("dinv", [P, S])
        dinv_out = keep("dinv_out", [P, S])
        self_common = keep("self_common", [P, S])
        all_common = keep("all_common", [P, S])
        max_common = keep("max_common", [P, 1])
        inv_max = keep("inv_max", [P, 1])

        a = region(RING * G * ROW)
        x1 = place(a, "x1", [P, RING, G, N], F32)
        W_hi = place(a, "W_hi", [P, S, N], F32R)
        W_lo = place(a + S * ROW, "W_lo", [P, S, N], F32R)
        b_ = region(S * ROW)
        noise = place(b_, "noise", [P, S, N], F32)
        y = place(b_, "y", [P, N], F32)
        y_hi = place(b_ + ROW, "y_hi", [P, 2, N], F32R)
        y_lo = place(b_ + 3 * ROW, "y_lo", [P, 2, N], F32R)
        scaled = place(b_ + 5 * ROW, "scaled", [P, 2, N], F32)
        adj_t = place(b_ + 4 * ROW, "adj_t", [P, S, N], BF16)
        c_ = region(4 * ROW)
        pairs = place(c_, "pairs", [P, 2, N, 2], F32)
        square = place(c_, "square", [P, 2, N], F32)
        weights = place(c_ + 2 * ROW, "weights", [P, 2, N], F32)
        adj = place(region(S * N * 2), "adj", [P, S, N], BF16)
        nmask = place(region(S * N * 2), "nmask", [P, S, N], BF16)
        x2 = place(region(XB * ROW), "x2", [P, XB, N], F32)
        hs = region(ROW)
        share = place(hs, "share", [P, N], F32)
        h = place(hs, "h", [P, N], F32)
        h_hi = place(region(ROW // 2), "h_hi", [P, N], F16)
        h_lo = place(region(ROW // 2), "h_lo", [P, N], F16)
        g_ = region(4 * ROW)
        avg = place(g_, "avg", [P, N], F32)
        avg_sq = place(g_ + ROW, "avg_sq", [P, N], F32)
        feats = place(g_ + 2 * ROW, "feats", [P, N], F32)
        result = place(g_, "result", [P, 2, N], F32)
        products = place(g_ + 2 * ROW, "products", [P, N], F32)
        dinv_row = place(g_ + 2 * ROW, "dinv_row", [P, N], F32)
        diag = place(g_ + 3 * ROW, "diag", [P, S, P], F32)
        assert top[0] <= nc.sbuf_usable_end

        ps = ctx.enter_context(nc.psum_tensor("ps", [P, 4, N], F32))
        SUM, COLS, ROWS, Y = 0, 1, 2, 3

        consts_ready = sem("consts_ready")
        consts_zero = sem("consts_zero")
        params_in = sem("params_in")
        w_hi_ready = sem("w_hi_ready")
        w_lo_ready = sem("w_lo_ready")
        w_turned = sem("w_turned")
        w_pow_step = sem("w_pow_step")
        w_cols_ready = sem("w_cols_ready")
        share_zero = sem("share_zero")
        x1_in = [[sem(f"x1_in{k}_{pair}") for pair in range(2)] for k in range(RING)]
        pairs_in = [sem(f"pairs_in{k}") for k in range(2)]
        noise_made = sem("noise_made")
        halves_ready = sem("halves_ready")
        mean_var_ready = sem("mean_var_ready")
        var_eps_ready = sem("var_eps_ready")
        stdev_ready = sem("stdev_ready")
        inv0_ready = sem("inv0_ready")
        newton_step = sem("newton_step")
        affine_ready = sem("affine_ready")
        norms_ready = sem("norms_ready")
        h1_ready = sem("h1_ready")
        pair_summed = [sem(f"pair_summed{pair}") for pair in range(2)]
        share_summed = sem("share_summed")
        sum_done = sem("sum_done")
        avg_ready = sem("avg_ready")
        avg_sq_ready = sem("avg_sq_ready")
        sumsq_done = sem("sumsq_done")
        col_v_ready = sem("col_v_ready")
        col_sqrt_ready = sem("col_sqrt_ready")
        col_step = sem("col_step")
        diag_ready = sem("diag_ready")
        row_done = sem("row_done")
        feats_ready = sem("feats_ready")
        sim_done = sem("sim_done")
        adj_ready = sem("adj_ready")
        sym_done = sem("sym_done")
        adj_t_ready = sem("adj_t_ready")
        nmask_offdiag = sem("nmask_offdiag")
        nmask_ready = sem("nmask_ready")
        common_done = sem("common_done")
        self_ready = sem("self_ready")
        square_all = sem("square_all")
        square_ready = sem("square_ready")
        degree_ready = sem("degree_ready")
        weights_ready = sem("weights_ready")
        W_hi_ready = sem("W_hi_ready")
        W_lo_ready = sem("W_lo_ready")
        max_ready = sem("max_ready")
        dinv_ready = sem("dinv_ready")
        dinv_row_ready = sem("dinv_row_ready")
        x2_in = [sem(f"x2_in{k}") for k in range(XB)]
        h_ready = sem("h_ready")
        h_hi_ready = sem("h_hi_ready")
        h_lo_ready = sem("h_lo_ready")
        y_done = sem("y_done")
        y_ready = sem("y_ready")
        y_hi_ready = sem("y_hi_ready")
        y_lo_ready = sem("y_lo_ready")
        agg_done = sem("agg_done")
        scaled_ready = sem("scaled_ready")
        result_ready = sem("result_ready")
        result_stored = [sem(f"result_stored{k}") for k in range(2)]

        def rows(t):
            return t.rearrange("p (c n) -> p c n", n=P)

        block = ctx.enter_context(nc.Block())

        @block.sync
        def _(sp):
            def load_pair(start, k, pair):
                sp.dma_start(x1[:, k, 2 * pair:2 * pair + 2], x_btn[:, ds(start, 2), :]).then_inc(x1_in[k][pair], 16)

            for k in range(RING):
                for pair in range(2):
                    load_pair(k * G + 2 * pair, k, pair)
                if k == 0:
                    sp.dma_start(w_in[:], weight).then_inc(params_in, 16)
                    sp.dma_start(bias_sb[:], bias_col).then_inc(params_in, 16)
            with sp.Fori(1, STEPS) as j:
                for k in range(RING):
                    g = (j - 1) * RING + k
                    for pair in range(2):
                        sp.wait_ge(pair_summed[pair], g + 1)
                        if pair == 0:
                            sp.wait_ge(share_summed, g + 1)
                        load_pair((g + RING) * G + 2 * pair, k, pair)
            for c in range(S):
                if c >= 2:
                    sp.wait_ge(noise_made, c - 1)
                sp.dma_start(pairs[:, c % 2], gumbel_rows[:, c]).then_inc(pairs_in[c % 2], 16)
            for k in range(XB):
                sp.dma_start(x2[:, k], x_btn[:, k]).then_inc(x2_in[k], 16)

            def store(b, parity):
                sp.wait_ge(result_ready, b + 1)
                sp.dma_start(out_btn[:, ds(b, 1), :], result[:, parity:parity + 1]).then_inc(result_stored[parity], 16)

            with sp.Fori(0, B // XB - 1) as i:
                b = i * XB
                for k in range(XB):
                    store(b + k, k % 2)
                    sp.dma_start(x2[:, k:k + 1], x_btn[:, ds(b + k + XB, 1), :]).then_inc(x2_in[k], 16)
            for k in range(XB):
                store(B - XB + k, k % 2)
            for k in range(2):
                sp.wait_ge(result_stored[k], 16 * (B // 2 + 1))

        @block.gpsimd
        def _(pool):
            pool.memset(ident[:], 0.0).then_inc(consts_zero, 1)
            pool.memset(ones[:], 1.0).then_inc(consts_ready, 1)
            pool.memset(zeros[:], 0.0).then_inc(consts_ready, 1)
            pool.wait_ge(consts_zero, 1)
            pool.affine_select(out=ident[:], in_=ident[:], compare_op=ALU.not_equal, fill=1.0, base=0,
                               pattern=[[-1, P]], channel_multiplier=1).then_inc(consts_ready, 1)
            pool.wait_ge(consts_ready, 3)
            pool.tensor_copy(ident_bf[:], ident[:]).then_inc(consts_ready, 1)
            for tile, value in ((c_eps, EPS), (c_neg, -1.0), (c_half, H_SCALE / 2), (c_three, 1.5 * H_SCALE)):
                pool.memset(tile[:], value).then_inc(consts_ready, 1)
            pool.memset(share[:], 0.0).then_inc(share_zero, 1)
            pool.wait_ge(consts_ready, 8)
            pool.wait_ge(share_zero, 1)

            with pool.Fori(0, STEPS) as j:
                for k in range(RING):
                    g = j * RING + k
                    mean, var = (mean_var[:, k % 2, :, n] for n in range(2))
                    scale, shift = (affine[:, k % 2, n] for n in range(2))
                    pool.wait_ge(mean_var_ready, (g + 1) * G)
                    pool.tensor_tensor(var_eps[:], var, c_eps[:], ALU.add).then_inc(var_eps_ready, 1)
                    pool.tensor_tensor(neg_mean[:], mean, c_neg[:], ALU.mult).then_inc(newton_step, 1)
                    pool.wait_ge(var_eps_ready, g + 1)
                    pool.tensor_tensor(var_half[:], var_eps[:], c_half[:], ALU.mult).then_inc(newton_step, 1)
                    pool.wait_ge(inv0_ready, g + 1)
                    pool.tensor_tensor(newton_a[:], inv0[:], inv0[:], ALU.mult).then_inc(newton_step, 1)
                    pool.wait_ge(newton_step, 6 * g + 3)
                    pool.tensor_tensor(newton_b[:], newton_a[:], var_half[:], ALU.mult).then_inc(newton_step, 1)
                    pool.wait_ge(newton_step, 6 * g + 4)
                    pool.tensor_tensor(newton_c[:], c_three[:], newton_b[:], ALU.subtract).then_inc(newton_step, 1)
                    pool.wait_ge(newton_step, 6 * g + 5)
                    pool.tensor_tensor(scale, newton_c[:], inv0[:], ALU.mult).then_inc(newton_step, 1)
                    pool.wait_ge(newton_step, 6 * g + 6)
                    pool.tensor_tensor(shift, neg_mean[:], scale, ALU.mult).then_inc(affine_ready, 1)
                    pool.wait_ge(h1_ready, g * G + 1)
                    pool.tensor_tensor(share[:], share[:], x1[:, k, 0], ALU.add).then_inc(share_summed, 1)

            for c in range(S):
                pool.wait_ge(pairs_in[c % 2], 16 * (c // 2 + 1))
                pool.tensor_tensor(noise[:, c], pairs[:, c % 2, :, 1], pairs[:, c % 2, :, 0],
                                   ALU.subtract).then_inc(noise_made, 1)

            def low_h(b):
                pool.wait_ge(h_hi_ready, b + 1)
                if not (isinstance(b, int) and b == 0):
                    pool.wait_ge(y_done, b)
                pool.tensor_tensor(h_lo[:], h[:], h_hi[:], ALU.subtract).then_inc(h_lo_ready, 1)

            def low_y(b, parity):
                pool.wait_ge(y_hi_ready, b + 1)
                if not (isinstance(b, int) and b < 2):
                    pool.wait_ge(agg_done, b - 1)
                pool.tensor_tensor(y_lo[:, parity], y[:], y_hi[:, parity].bitcast(F32),
                                   ALU.subtract).then_inc(y_lo_ready, 1)

            low_h(0)
            for s in range(S):
                if s == S - 1:
                    pool.wait_ge(self_ready, S)
                    pool.partition_all_reduce(all_common[:], self_common[:], P, RMAX).then_inc(max_ready, 1)
                pool.wait_ge(W_hi_ready, s + 1)
                pool.tensor_tensor(W_lo[:, s], weights[:, s % 2], W_hi[:, s].bitcast(F32),
                                   ALU.subtract).then_inc(W_lo_ready, 1)
            for b in range(3):
                low_h(b + 1)
                low_y(b, b % 2)
            with pool.Fori(0, B // XB - 1) as i:
                b = i * XB + 3
                for k in range(XB):
                    low_h(b + k + 1)
                    low_y(b + k, (3 + k) % 2)
            low_y(B - 1, (B - 1) % 2)

        @block.scalar
        def _(act):
            act.wait_ge(w_turned, 2)
            act.copy(w_hi[:], ps[:, Y, 0:P]).then_inc(w_hi_ready, 1)

            def stdev_of(g):
                act.wait_ge(var_eps_ready, g + 1)
                act.activation(stdev[:], var_eps[:], ACT.Sqrt).then_inc(stdev_ready, 1)

            def h1(g, k, q):
                act.activation(x1[:, k, q], x1[:, k, q], ACT.Relu, scale=affine[:, k % 2, 0, q:q + 1],
                               bias=affine[:, k % 2, 1, q:q + 1]).then_inc(h1_ready, 1)

            def h1_group(j, k, last=False):
                g = j * RING + k
                act.wait_ge(affine_ready, g + 1)
                for q in range(G):
                    if q == G - 1 and not last:
                        stdev_of(g + 1)
                    h1(g, k, q)

            stdev_of(0)
            with act.Fori(0, STEPS - 1) as j:
                for k in range(RING):
                    h1_group(j, k)
            for k in range(RING):
                h1_group(STEPS - 1, k, last=(k == RING - 1))

            act.wait_ge(sum_done, 1)
            act.activation(avg_sq[:], ps[:, SUM], ACT.Square, scale=1.0 / (B * H_SCALE)).then_inc(avg_sq_ready, 1)
            act.activation(avg[:], ps[:, SUM], ACT.Copy, scale=1.0 / (B * H_SCALE)).then_inc(avg_ready, 1)
            act.wait_ge(col_v_ready, 1)
            act.activation(col_sqrt[:], col_v[:], ACT.Sqrt).then_inc(col_sqrt_ready, 1)

            def high_h(b, slot, turn):
                act.wait_ge(x2_in[slot], 16 * (turn + 1))
                if not (isinstance(b, int) and b == 0):
                    act.wait_ge(h_lo_ready, b)
                scale, shift = (norms[:, ds(turn, 1), n, slot:slot + 1] for n in range(2))
                act.activation(h[:], x2[:, slot], ACT.Relu, scale=scale, bias=shift).then_inc(h_ready, 1)
                act.wait_ge(h_ready, b + 1)
                if not (isinstance(b, int) and b == 0):
                    act.wait_ge(y_done, b)
                act.copy(h_hi[:], h[:]).then_inc(h_hi_ready, 1)

            def high_y(b, parity):
                act.wait_ge(y_ready, b + 1)
                if not (isinstance(b, int) and b < 2):
                    act.wait_ge(agg_done, b - 1)
                act.copy(y_hi[:, parity], y[:]).then_inc(y_hi_ready, 1)

            act.wait_ge(norms_ready, B // G)
            high_h(0, 0, 0)
            for s in range(S):
                act.wait_ge(sym_done, s + 1)
                act.copy(adj_t[:, s], ps[:, 2 + s % 2]).then_inc(adj_t_ready, 1)
            for s in range(S):
                act.wait_ge(self_ready, s + 1)
                if s >= 2:
                    act.wait_ge(weights_ready, s - 1)
                    act.wait_ge(degree_ready, s - 1)
                act.activation(square[:, s % 2], ps[:, s % 2], ACT.Square).then_inc(square_all, 1)
                if s:
                    act.wait_ge(weights_ready, s)
                    act.copy(W_hi[:, s - 1], weights[:, (s - 1) % 2]).then_inc(W_hi_ready, 1)
            act.wait_ge(col_v_ready, 2)
            act.activation(col_sqrt[:], col_v[:], ACT.Sqrt).then_inc(col_sqrt_ready, 1)
            act.wait_ge(weights_ready, S)
            act.copy(W_hi[:, S - 1], weights[:, (S - 1) % 2]).then_inc(W_hi_ready, 1)
            high_y(0, 0)
            for b in range(1, 4):
                high_h(b, b, 0)
                if b > 1:
                    high_y(b - 1, (b - 1) % 2)
                if b == 1:
                    act.wait_ge(row_done, 2)
                    act.copy(dinv_row[:], ps[:, ROWS]).then_inc(dinv_row_ready, 1)
            with act.Fori(1, B // XB) as i:
                for k in range(XB):
                    b = i * XB + k
                    high_h(b, k, i)
                    high_y(b - 1, (k + 1) % 2)
            high_y(B - 1, (B - 1) % 2)

        @block.vector
        def _(dve):
            def refine(v, root, inv, tmp, out_, sem_, n0):
                dve.reciprocal(inv, root).then_inc(sem_, 1)
                dve.wait_ge(sem_, n0 + 1)
                dve.tensor_tensor(tmp[0], inv, inv, ALU.mult).then_inc(sem_, 1)
                dve.wait_ge(sem_, n0 + 2)
                dve.tensor_tensor(tmp[1], tmp[0], v, ALU.mult).then_inc(sem_, 1)
                dve.wait_ge(sem_, n0 + 3)
                dve.tensor_scalar(tmp[2], tmp[1], -0.5, 1.5, ALU.mult, ALU.add).then_inc(sem_, 1)
                dve.wait_ge(sem_, n0 + 4)
                dve.tensor_tensor(out_, tmp[2], inv, ALU.mult).then_inc(sem_, 1)
                dve.wait_ge(sem_, n0 + 5)

            dve.wait_ge(w_turned, 1)
            dve.tensor_reduce(w_max[:], ps[:, Y, 0:P], AX_X, ALU.max, apply_absolute_value=True).then_inc(w_pow_step, 1)
            dve.wait_ge(w_pow_step, 1)
            dve.tensor_scalar(w_pow[:], w_max[:], W_MIN, None, ALU.max).then_inc(w_pow_step, 1)
            dve.wait_ge(w_pow_step, 2)
            dve.tensor_scalar(w_pow_inv[:].bitcast(I32), w_pow[:].bitcast(I32), EXPONENT, None,
                              ALU.bitwise_and).then_inc(w_pow_step, 1)
            dve.wait_ge(w_pow_step, 3)
            dve.tensor_scalar(unscale[:], w_pow_inv[:], 1.0 / (W_TOP * H_SCALE), None, ALU.mult).then_inc(w_pow_step, 1)
            dve.reciprocal(w_pow[:], w_pow_inv[:]).then_inc(w_pow_step, 1)
            dve.wait_ge(w_pow_step, 5)
            dve.tensor_scalar(w_cols[:], ps[:, Y, 0:P], w_pow[:, 0:1], W_TOP, ALU.mult, ALU.mult).then_inc(w_cols_ready, 1)
            dve.wait_ge(w_hi_ready, 1)
            dve.tensor_tensor(w_lo[:], ps[:, Y, 0:P], w_hi[:], ALU.subtract).then_inc(w_lo_ready, 1)

            def invert(g):
                dve.wait_ge(stdev_ready, g + 1)
                dve.reciprocal(inv0[:], stdev[:]).then_inc(inv0_ready, 1)

            def note(g, parity):
                dve.wait_ge(affine_ready, g + 1)
                dve.tensor_scalar(norms[:, ds(g, 1)], affine[:, parity:parity + 1], 1.0, None,
                                  ALU.mult).then_inc(norms_ready, 1)

            def statistics(j, k, first=False):
                g = j * RING + k
                for q in range(G):
                    if q % 2 == 0:
                        dve.wait_ge(x1_in[k][q // 2], 16 * (j + 1))
                    dve.bn_stats(halves[:, k % 2, q, 0], x1[:, k, q, 0:H]).then_inc(halves_ready, 1)
                    if q:
                        dve.wait_ge(halves_ready, (g * G + q) * 2)
                    dve.bn_stats(halves[:, k % 2, q, 1], x1[:, k, q, H:N]).then_inc(halves_ready, 1)
                    if q:
                        dve.bn_aggr(mean_var[:, k % 2, q - 1], halves[:, k % 2, q - 1]).then_inc(mean_var_ready, 1)
                    if q == 0 and not first:
                        invert(g - 1)
                    if q == G - 1 and not first:
                        note(g - 1, (k - 1) % 2)
                dve.wait_ge(halves_ready, (g + 1) * G * 2)
                dve.memset(waiting[:], 0.0)
                dve.bn_aggr(mean_var[:, k % 2, G - 1], halves[:, k % 2, G - 1]).then_inc(mean_var_ready, 1)

            for k in range(RING):
                statistics(0, k, first=(k == 0))
            with dve.Fori(1, STEPS) as j:
                for k in range(RING):
                    statistics(j, k)
            invert(B // G - 1)
            note(B // G - 1, 1)

            dve.wait_ge(sumsq_done, 1)
            dve.tensor_scalar(col_v[:], ps[:, COLS, 0:S], NORM_MIN ** 2, None, ALU.max).then_inc(col_v_ready, 1)
            dve.wait_ge(col_sqrt_ready, 1)
            cols = (col_a[:], col_b[:], col_c[:])
            refine(col_v[:], col_sqrt[:], col_inv[:], cols, inv_norm[:], col_step, 0)
            ident_rows = ident[:].unsqueeze(1).to_broadcast([P, S, P])
            dve.wait_ge(consts_ready, 8)
            dve.tensor_tensor(diag[:], ident_rows, inv_norm[:].unsqueeze(2).to_broadcast([P, S, P]),
                              ALU.mult).then_inc(diag_ready, 1)
            dve.wait_ge(row_done, 1)
            dve.wait_ge(avg_ready, 1)
            dve.tensor_tensor(feats[:], avg[:], ps[:, ROWS], ALU.mult).then_inc(feats_ready, 1)

            dve.wait_ge(noise_made, S)
            for s in range(S):
                dve.wait_ge(sim_done, s + 1)
                dve.tensor_tensor(adj[:, s], ps[:, s % 2], noise[:, s], ALU.is_gt).then_inc(adj_ready, 1)
            for s in range(S):
                node = slice(s * P, s * P + P)
                dve.wait_ge(adj_t_ready, s + 1)
                dve.tensor_tensor(nmask[:, s], adj[:, s], adj_t[:, s], ALU.max).then_inc(nmask_offdiag, 1)
                dve.wait_ge(nmask_offdiag, s + 1)
                dve.tensor_tensor(nmask[:, s, node], nmask[:, s, node], ident_bf[:], ALU.max).then_inc(nmask_ready, 1)
            for s in range(S):
                node = slice(s * P, s * P + P)
                dve.wait_ge(common_done, s + 1)
                dve.tensor_reduce(self_common[:, s:s + 1], ps[:, s % 2, node], AX_X, ALU.max).then_inc(self_ready, 1)
                dve.wait_ge(square_all, s + 1)
                dve.scalar_tensor_tensor(out=square[:, s % 2, node], in0=square[:, s % 2, node], scalar=1.0,
                                         in1=square[:, s % 2, node], op0=ALU.is_gt,
                                         op1=ALU.mult).then_inc(square_ready, 1)
                dve.wait_ge(square_ready, s + 1)
                dve.tensor_tensor_reduce(products[:], square[:, s % 2], adj_t[:, s], 1.0, 0.0, ALU.mult, ALU.add,
                                         degree[:, s:s + 1]).then_inc(degree_ready, 1)
                if s >= 2:
                    dve.wait_ge(W_lo_ready, s - 1)
                dve.tensor_tensor(weights[:, s % 2], square[:, s % 2], adj[:, s], ALU.mult).then_inc(weights_ready, 1)

            dve.wait_ge(max_ready, 1)
            dve.tensor_reduce(max_common[:], all_common[:], AX_X, ALU.max).then_inc(col_step, 1)
            dve.wait_ge(col_step, 6)
            dve.reciprocal(inv_max[:], max_common[:]).then_inc(col_step, 1)
            dve.wait_ge(col_step, 7)
            dve.wait_ge(degree_ready, S)
            dve.tensor_scalar(degree_n[:], degree[:], inv_max[:, 0:1], None, ALU.mult).then_inc(col_step, 1)
            dve.wait_ge(col_step, 8)
            dve.tensor_scalar(col_v[:], degree_n[:], DEG_MIN, None, ALU.max).then_inc(col_v_ready, 1)
            dve.tensor_scalar(has_edge[:], degree_n[:], 0.0, None, ALU.is_gt).then_inc(col_step, 1)
            dve.wait_ge(col_sqrt_ready, 2)
            refine(col_v[:], col_sqrt[:], col_inv[:], cols, inv_norm[:], col_step, 9)
            dve.tensor_tensor(dinv[:], inv_norm[:], has_edge[:], ALU.mult).then_inc(dinv_ready, 1)
            dve.wait_ge(dinv_ready, 1)
            dinv_rows = dinv[:].unsqueeze(2).to_broadcast([P, S, P])

            def scale_y(b):
                dve.wait_ge(y_done, b + 1)
                if not (isinstance(b, int) and b == 0):
                    dve.wait_ge(y_hi_ready, b)
                    dve.wait_ge(y_lo_ready, b)
                dve.tensor_tensor(rows(y[:]), rows(ps[:, Y]), dinv_rows, ALU.mult).then_inc(y_ready, 1)

            def finish(b, parity, slot, stored):
                dve.wait_ge(agg_done, b + 1)
                dve.scalar_tensor_tensor(out=scaled[:, parity], in0=ps[:, parity], scalar=unscale[:, 0:1],
                                         in1=dinv_row[:], op0=ALU.mult, op1=ALU.mult).then_inc(scaled_ready, 1)
                dve.wait_ge(scaled_ready, b + 1)
                dve.wait_ge(result_stored[parity], stored)
                dve.scalar_tensor_tensor(out=result[:, parity], in0=scaled[:, parity], scalar=bias_sb[:, 0:1],
                                         in1=x2[:, slot], op0=ALU.add, op1=ALU.add).then_inc(result_ready, 1)

            dve.nop().then_inc(result_stored[0], 16)
            dve.nop().then_inc(result_stored[1], 16)
            scale_y(0)
            dve.tensor_scalar(dinv_out[:], dinv[:], inv_max[:, 0:1], None, ALU.mult).then_inc(dinv_ready, 1)
            dve.wait_ge(dinv_ready, 2)
            dve.tensor_tensor(diag[:], ident_rows, dinv_out[:].unsqueeze(2).to_broadcast([P, S, P]),
                              ALU.mult).then_inc(diag_ready, 1)
            scale_y(1)
            dve.wait_ge(dinv_row_ready, 1)
            for b in range(3):
                if b:
                    scale_y(b + 1)
                finish(b, b % 2, b, 16 * (b // 2 + 1))
            with dve.Fori(1, B // XB) as i:
                for k in range(XB):
                    b = i * XB + k
                    scale_y(b)
                    finish(b - 1, (k + 1) % 2, (k - 1) % XB, 16 * (i * 2 + (k - 1) // 2 + 1))
            finish(B - 1, (B - 1) % 2, XB - 1, 16 * ((B - 1) // 2 + 1))

        @block.tensor
        def _(pe):
            def turn(src):
                pe.transpose(ps[:, Y, 0:P], src, ident[:]).then_inc(w_turned, 1)

            pe.wait_ge(consts_ready, 4)
            for half in range(2):
                pe.matmul(ps[:, SUM, half * H:half * H + H], ident[:], zeros[:], start=True, stop=False)
            pe.wait_ge(params_in, 32)
            turn(w_in[:])
            pe.wait_ge(w_cols_ready, 1)
            turn(w_cols[:])
            with pe.Fori(0, STEPS) as j:
                for k in range(RING):
                    g = j * RING + k
                    for q in range(1, G):
                        pe.wait_ge(h1_ready, g * G + q + 1)
                        for half in range(2):
                            mm = pe.matmul(ps[:, SUM, half * H:half * H + H], ident[:],
                                           x1[:, k, q, half * H:half * H + H], start=False, stop=False)
                        if q % 2:
                            mm.then_inc(pair_summed[q // 2], 1)
            pe.wait_ge(share_summed, B // G)
            for half in range(2):
                mm = pe.matmul(ps[:, SUM, half * H:half * H + H], ident[:], share[:, half * H:half * H + H],
                               start=False, stop=True)
            mm.then_inc(sum_done, 1)

            pe.wait_ge(avg_sq_ready, 1)
            for s in range(S):
                mm = pe.matmul(ps[:, COLS, s:s + 1], avg_sq[:, s * P:s * P + P], ones[:, 0:1], start=True, stop=True)
            mm.then_inc(sumsq_done, 1)

            def spread_diag(n):
                pe.wait_ge(diag_ready, n)
                for half in range(2):
                    mm = pe.matmul(ps[:, ROWS, half * H:half * H + H], ones[:],
                                   diag[:, half * (S // 2):(half + 1) * (S // 2), :], start=True, stop=True)
                mm.then_inc(row_done, 1)

            spread_diag(1)
            pe.wait_ge(feats_ready, 1)
            for s in range(S):
                if s >= 2:
                    pe.wait_ge(adj_ready, s - 1)
                for half in range(2):
                    mm = pe.matmul(ps[:, s % 2, half * H:half * H + H], feats[:, s * P:s * P + P],
                                   feats[:, half * H:half * H + H], start=True, stop=True)
                mm.then_inc(sim_done, 1)
            pe.wait_ge(adj_ready, S)
            for s in range(S):
                if s >= 2:
                    pe.wait_ge(adj_t_ready, s - 1)
                for d in range(S):
                    mm = pe.matmul(ps[:, 2 + s % 2, d * P:d * P + P], adj[:, d, s * P:s * P + P], ident_bf[:],
                                   start=True, stop=True)
                mm.then_inc(sym_done, 1)
            pe.wait_ge(nmask_ready, S)
            for s in range(S):
                if s >= 2:
                    pe.wait_ge(square_all, s - 1)
                for c in range(S):
                    for half in range(2):
                        mm = pe.matmul(ps[:, s % 2, half * H:half * H + H], nmask[:, c, s * P:s * P + P],
                                       nmask[:, c, half * H:half * H + H], start=(c == 0), stop=(c == S - 1))
                mm.then_inc(common_done, 1)

            def project(b):
                pe.wait_ge(h_hi_ready, b + 1)
                pe.wait_ge(h_lo_ready, b + 1)
                if not (isinstance(b, int) and b == 0):
                    pe.wait_ge(y_ready, b)
                for s in range(S):
                    node = slice(s * P, s * P + P)
                    pe.matmul(ps[:, Y, node], h_hi[:, node], w_hi[:], start=True, stop=False)
                    pe.matmul(ps[:, Y, node], h_hi[:, node], w_lo[:], start=False, stop=False)
                    mm = pe.matmul(ps[:, Y, node], h_lo[:, node], w_hi[:], start=False, stop=True)
                mm.then_inc(y_done, 1)

            def aggregate(b, parity, first=False):
                pe.wait_ge(y_hi_ready, b + 1)
                if not (isinstance(b, int) and b < 2):
                    pe.wait_ge(scaled_ready, b - 1)
                for s in range(S):
                    if first:
                        pe.wait_ge(W_lo_ready, s + 1)
                    for W_part in (W_hi, W_lo):
                        for half in range(2):
                            pe.matmul(ps[:, parity, half * H:half * H + H], y_hi[:, parity, s * P:s * P + P],
                                      W_part[:, s, half * H:half * H + H],
                                      start=(s == 0 and W_part is W_hi), stop=False)
                pe.wait_ge(y_lo_ready, b + 1)
                for s in range(S):
                    for half in range(2):
                        mm = pe.matmul(ps[:, parity, half * H:half * H + H], y_lo[:, parity, s * P:s * P + P],
                                       W_hi[:, s, half * H:half * H + H], start=False, stop=(s == S - 1))
                mm.then_inc(agg_done, 1)

            pe.wait_ge(w_lo_ready, 1)
            project(0)
            project(1)
            pe.wait_ge(square_all, S)
            aggregate(0, 0, first=True)
            spread_diag(2)
            with pe.Fori(0, (B - 2) // 2) as i:
                b = i * 2 + 1
                for k in range(2):
                    project(b + k + 1)
                    aggregate(b + k, (1 + k) % 2)
            aggregate(B - 1, (B - 1) % 2)


_INS = ['x', 'adj', 'L0_gnn_bias', 'L0_gnn_gumbel']
_OUTS = [((64, 128, 1024), 'float32')]


def kernel(**inputs):
    import numpy as _np
    import concourse.bacc as _bacc
    from concourse import mybir as _mybir
    from concourse.bass_utils import run_bass_kernel_spmd as _run

    nc = _bacc.Bacc("TRN2", target_bir_lowering=False, num_devices=1)
    arrays, args = {}, []
    for name in _INS:
        a = _np.ascontiguousarray(inputs[name])
        arrays[f"in_{name}_dram"] = a
        args.append(nc.dram_tensor(f"in_{name}_dram", a.shape, _mybir.dt.from_np(a.dtype), kind="ExternalInput").ap())
    for i, (shape, dtype) in enumerate(_OUTS):
        dt = _mybir.dt.from_np(_np.dtype(dtype))
        args.append(nc.dram_tensor(f"out_{i}_dram", shape, dt, kind="ExternalOutput").ap())
    gnn_program(nc, *args)
    r = _run(nc, [arrays], core_ids=[0])
    got = tuple(r.results[0][f"out_{i}_dram"] for i in range(len(_OUTS)))
    return got[0]
```

```python
from contextlib import ExitStack

import concourse.bass as bass
from concourse import mybir

ALU = mybir.AluOpType
ACT = mybir.ActivationFunctionType
F32 = mybir.dt.float32
F32R = mybir.dt.float32r
BF16 = mybir.dt.bfloat16
F16 = mybir.dt.float16
I32 = mybir.dt.int32
AX_X = mybir.AxisListType.X
RMAX = bass.bass_isa.ReduceOp.max
ds = bass.ds

EPS = 1e-5
NORM_MIN = 1e-12
DEG_MIN = 1e-6
H_SCALE = 1024.0
W_TOP = 2.0 ** 14
W_MIN = 1e-30
EXPONENT = 0x7F800000

B11, B21, B22, T3, T2, T1, T4 = range(7)
P1, P2, P6, P5, P7, P3, P4 = range(7)
RIGHT = (B11, B21, T2, T1, T3, B22, T4)
BANKS = 4
A11, A12, A21, A22, S1, S2 = range(6)
LEFT = (A11, A12, S2, S1, A21, A12, A22)
NUM = 7


def gnn_program(nc, x, weight, bias, gumbel, out):
    B, T, N = x.shape
    P = 128
    S = N // P
    H = N // 2
    G = 4
    RING = 4
    STEPS = B // G // RING
    CHUNKS_STEP = S // STEPS
    XB = 4
    PAIRS = B // 2
    KS = S // 2
    LAST = KS - 1
    assert S % 2 == 0 and B >= 4 * XB
    assert T == P and B % (G * RING) == 0 and S % STEPS == 0 and CHUNKS_STEP == 2 and B % XB == 0

    x_btn = x.rearrange("b t n -> t b n")
    out_btn = out.rearrange("b t n -> t b n")
    gumbel_rows = gumbel.rearrange("(c p n) k -> p c n k", p=P, n=N)
    bias_col = bias.rearrange("(t a) -> t a", a=1)

    with ExitStack() as ctx:
        top = [16512]

        def place(offset, name, shape, dtype):
            return nc.alloc_sbuf_tensor_at(name, shape, dtype, offset=offset)

        def region(size):
            start = top[0]
            top[0] += size
            return start

        def keep(name, shape, dtype=F32):
            size = 1
            for s in shape[1:]:
                size *= s
            return place(region(-(-size * (2 if dtype in (BF16, F16) else 4) // 32) * 32), name, shape, dtype)

        def sem(name):
            return ctx.enter_context(nc.semaphore(name))

        ROW = 4 * N

        ident = keep("ident", [P, P])
        ident_bf = keep("ident_bf", [P, P], BF16)
        ones = keep("ones", [P, P])
        w_in = keep("w_in", [P, P])
        w_cols = keep("w_cols", [P, P])
        w_hi = keep("w_hi", [P, P], F16)
        w_lo = keep("w_lo", [P, P], F16)
        w_max = keep("w_max", [P, 1])
        w_pow = keep("w_pow", [P, 1])
        w_pow_inv = keep("w_pow_inv", [P, 1])
        unscale = keep("unscale", [P, 1])
        bias_sb = keep("bias_sb", [P, 1])
        halves = keep("halves", [P, 2, G, 2, 6])
        mean_var = keep("mean_var", [P, 2, G, 2])
        waiting = keep("waiting", [P, 1])
        c_eps, c_neg, c_half, c_three = (keep(f"c_{n}", [P, G]) for n in ("eps", "neg", "half", "three"))
        var_eps = keep("var_eps", [P, G])
        var_half = keep("var_half", [P, G])
        neg_mean = keep("neg_mean", [P, G])
        stdev = keep("stdev", [P, G])
        inv0 = keep("inv0", [P, G])
        newton_a = keep("newton_a", [P, G])
        newton_b = keep("newton_b", [P, G])
        newton_c = keep("newton_c", [P, G])
        affine = keep("affine", [P, 2, 2, G])
        norms = keep("norms", [P, B // G, 2, G])
        col_v = keep("col_v", [P, S])
        col_sqrt = keep("col_sqrt", [P, S])
        col_inv = keep("col_inv", [P, S])
        col_a = keep("col_a", [P, S])
        col_b = keep("col_b", [P, S])
        col_c = keep("col_c", [P, S])
        inv_norm = keep("inv_norm", [P, S])
        degree = keep("degree", [P, S])
        degree_n = keep("degree_n", [P, S])
        has_edge = keep("has_edge", [P, S])
        dinv = keep("dinv", [P, S])
        dinv_out = keep("dinv_out", [P, S])
        self_common = keep("self_common", [P, S])
        all_common = keep("all_common", [P, S])
        max_common = keep("max_common", [P, 1])
        inv_max = keep("inv_max", [P, 1])

        r = region(28 * ROW)
        x1 = place(r, "x1", [P, RING, G, N], F32)
        noise = place(r + 16 * ROW, "noise", [P, S, N], F32)
        pairs = place(r + 24 * ROW, "pairs", [P, 2, N, 2], F32)
        right_hi = place(r, "right_hi", [P, KS, NUM, H], F32R)
        right_lo = place(r + 14 * ROW, "right_lo", [P, KS, NUM, H], F32R)
        first_low0 = place(r + 21 * ROW // 2, "first_low0", [P, N], F16)
        first_high1 = place(r + 11 * ROW, "first_high1", [P, N], F16)
        first_low1 = place(r + 23 * ROW // 2, "first_low1", [P, N], F16)
        first_h = place(r + 49 * ROW // 2, "first_h", [P, N], F32)
        first_high0 = place(r + 51 * ROW // 2, "first_high0", [P, N], F16)
        q = region(22 * ROW)
        share = place(q, "share", [P, N], F32)
        adj_t = place(q, "adj_t", [P, S, N], BF16)
        adj = place(q + 4 * ROW, "adj", [P, S, N], BF16)
        left = place(q, "left", [P, NUM, 2, H], F32R)
        wide = [place(q + row * ROW, f"wide{row}", [P, S, P], F32) for row in (11, 6)]
        zeros = place(q + 8 * ROW, "zeros", [P, H], F32)
        avg = place(q + 8 * ROW, "avg", [P, N], F32)
        avg_sq = place(q + 9 * ROW, "avg_sq", [P, N], F32)
        feats = place(q + 10 * ROW, "feats", [P, N], F32)
        feats_hi = place(q + 9 * ROW, "feats_hi", [P, N], F32R)
        feats_lo = place(q + 11 * ROW, "feats_lo", [P, N], F32R)
        nmask = place(q + 8 * ROW, "nmask", [P, S, N], BF16)
        y = place(q + 8 * ROW, "y", [P, 6, H], F32)
        u = place(q + 11 * ROW, "u", [P, 2, H], F32)
        total = place(q + 12 * ROW, "total", [P, N], F32)
        square = place(q + 12 * ROW, "square", [P, 2, N], F32)
        h_hi = place(q + 12 * ROW, "h_hi", [P, 2, N], F16)
        h_lo = place(q + 13 * ROW, "h_lo", [P, 2, N], F16)
        products = place(q + 14 * ROW, "products", [P, N], F32)
        h = place(q + 14 * ROW, "h", [P, N], F32)
        edges = [place(start, f"edges{k}", [P, 2, 2, H], F32) for k, start in enumerate((r + 12 * ROW, q + 15 * ROW))]
        sums = [place(start, f"sums{k}", [P, 4, H], F32) for k, start in enumerate((r + 26 * ROW, q + 17 * ROW))]
        dinv_row = place(q + 16 * ROW, "dinv_row", [P, N], F32)
        result = place(q + 17 * ROW, "result", [P, 2, N], F32)
        x2 = [place(q + row * ROW, f"x2_{k}", [P, N], F32) for k, row in enumerate((19, 20, 7, 21))]
        assert top[0] <= nc.sbuf_usable_end

        ps = ctx.enter_context(nc.psum_tensor("ps", [P, 4, N], F32))
        SUM, COLS, ROWS, Y = 0, 1, 2, 3

        def bank(k):
            return ps[:, k % BANKS // 2, k % 2 * H:k % 2 * H + H]

        def y_bank(e):
            return ps[:, 2 + e]

        def place_of(s):
            return s % 2 * KS + s // 2

        consts_ready = sem("consts_ready")
        consts_zero = sem("consts_zero")
        params_in = sem("params_in")
        w_hi_ready = sem("w_hi_ready")
        w_lo_ready = sem("w_lo_ready")
        w_turned = sem("w_turned")
        w_pow_step = sem("w_pow_step")
        w_cols_ready = sem("w_cols_ready")
        share_zero = sem("share_zero")
        x1_in = [[sem(f"x1_in{k}_{pair}") for pair in range(2)] for k in range(RING)]
        pairs_in = [sem(f"pairs_in{c}") for c in range(S)]
        noise_pool = sem("noise_pool")
        noise_dve = sem("noise_dve")
        halves_ready = sem("halves_ready")
        mean_var_ready = sem("mean_var_ready")
        var_eps_ready = sem("var_eps_ready")
        stdev_ready = sem("stdev_ready")
        inv0_ready = sem("inv0_ready")
        newton_step = sem("newton_step")
        affine_ready = sem("affine_ready")
        norms_ready = sem("norms_ready")
        h1_ready = sem("h1_ready")
        pair_summed = [sem(f"pair_summed{pair}") for pair in range(2)]
        share_summed = sem("share_summed")
        sum_done = sem("sum_done")
        total_ready = sem("total_ready")
        avg_ready = sem("avg_ready")
        avg_sq_ready = sem("avg_sq_ready")
        sumsq_done = sem("sumsq_done")
        col_v_ready = sem("col_v_ready")
        col_sqrt_ready = sem("col_sqrt_ready")
        col_step = sem("col_step")
        row_done = sem("row_done")
        wide_ready = sem("wide_ready")
        feats_ready = sem("feats_ready")
        sim_done = sem("sim_done")
        adj_ready = sem("adj_ready")
        sym_done = sem("sym_done")
        adj_t_ready = sem("adj_t_ready")
        nmask_offdiag = sem("nmask_offdiag")
        nmask_ready = sem("nmask_ready")
        common_done = sem("common_done")
        self_ready = sem("self_ready")
        square_all = sem("square_all")
        square_ready = sem("square_ready")
        degree_ready = sem("degree_ready")
        weights_ready = sem("weights_ready")
        sums_ready = sem("sums_ready")
        right_hi_ready = [sem(f"right_hi_ready{k}") for k in range(2)]
        right_lo_ready = [sem(f"right_lo_ready{k}") for k in range(2)]
        right_lo_last = sem("right_lo_last")
        max_ready = sem("max_ready")
        dinv_ready = sem("dinv_ready")
        dinv_row_ready = sem("dinv_row_ready")
        x2_in = [sem(f"x2_in{k}") for k in range(XB)]
        h_ready = sem("h_ready")
        h_hi_ready = sem("h_hi_ready")
        h_lo_ready = sem("h_lo_ready")
        y_done = sem("y_done")
        y_ready = sem("y_ready")
        s_ready = sem("s_ready")
        left_hi_ready = sem("left_hi_ready")
        left_lo_ready = sem("left_lo_ready")
        product_done = sem("product_done")
        p1_copied = sem("p1_copied")
        u2_ready = sem("u2_ready")
        u3_ready = sem("u3_ready")
        u4_ready = sem("u4_ready")
        c_ready = sem("c_ready")
        scaled_ready = sem("scaled_ready")
        result_ready = [sem(f"result_ready{k}") for k in range(2)]
        result_stored = [sem(f"result_stored{k}") for k in range(2)]

        def gumbel_of(c):
            if c < 2:
                return pairs[:, c]
            return x1[:, (c - 2) // 2, c % 2 * 2:c % 2 * 2 + 2].rearrange("p q n -> p (q n)").rearrange(
                "p (n k) -> p n k", k=2)

        NOISE_POOL = [c for c in range(S) if c % 2 == 0 or c == S - 1]
        NOISE_DVE = [c for c in range(S) if c not in NOISE_POOL]

        def make_noise(eng, c, sem_):
            eng.wait_ge(pairs_in[c], 16)
            eng.tensor_tensor(noise[:, c], gumbel_of(c)[:, :, 1], gumbel_of(c)[:, :, 0], ALU.subtract).then_inc(sem_, 1)

        def right_part(i, part):
            start, n = ((B11, 1), (B21, 2), (T3, 2), (T1, 2))[part]
            of = (edges[i % 2][:, 0, 0:1], edges[i % 2][:, 1], sums[i % 2][:, 0:2], sums[i % 2][:, 2:4])[part]
            return right_hi[:, i, start:start + n], right_lo[:, i, start:start + n], of

        def right_turn(i, part):
            return part // 2, 2 * i + part % 2 + 1

        def rows_of_half(t):
            return t.rearrange("p (m n) -> p m n", n=H)

        def rows(t):
            return t.rearrange("p (c n) -> p c n", n=P)

        block = ctx.enter_context(nc.Block())

        @block.sync
        def _(sp):
            def load_pair(start, k, pair):
                sp.dma_start(x1[:, k, 2 * pair:2 * pair + 2], x_btn[:, ds(start, 2), :]).then_inc(x1_in[k][pair], 16)

            for k in range(RING):
                for pair in range(2):
                    load_pair(k * G + 2 * pair, k, pair)
                if k == 0:
                    sp.dma_start(w_in[:], weight).then_inc(params_in, 16)
                    sp.dma_start(bias_sb[:], bias_col).then_inc(params_in, 16)
            with sp.Fori(1, STEPS) as j:
                for k in range(RING):
                    g = (j - 1) * RING + k
                    for pair in range(2):
                        sp.wait_ge(pair_summed[pair], g + 1)
                        if pair == 0:
                            sp.wait_ge(share_summed, g + 1)
                        load_pair((g + RING) * G + 2 * pair, k, pair)
            for c in range(S):
                if c >= 2:
                    done = B // G - RING + (c - 2) // 2 + 1
                    sp.wait_ge(pair_summed[c % 2], done)
                    if c % 2 == 0:
                        sp.wait_ge(share_summed, done)
                sp.dma_start(gumbel_of(c), gumbel_rows[:, c]).then_inc(pairs_in[c], 16)
            def load(b, slot):
                sp.dma_start(x2[slot].rearrange("p (b n) -> p b n", b=1), x_btn[:, ds(b, 1), :]).then_inc(x2_in[slot], 16)

            for k in (0, 1, 3):
                load(k, k)
            sp.wait_ge(weights_ready, S)
            load(2, 2)

            def store(b, turn, parity):
                sp.wait_ge(result_ready[parity], turn)
                sp.dma_start(out_btn[:, ds(b, 1), :], result[:, parity:parity + 1]).then_inc(result_stored[parity], 16)

            with sp.Fori(0, B // XB - 1) as i:
                b = i * XB
                for k in range(XB):
                    sp.wait_ge(result_ready[k % 2], i * 4 + (k // 2 * 2 + 2))
                    load(b + k + XB, k)
                    store(b + k, i * 4 + (k // 2 * 2 + 2), k % 2)
            for k in range(XB):
                store(B - XB + k, B - XB + k // 2 * 2 + 2, k % 2)
            for k in range(2):
                sp.wait_ge(result_stored[k], 16 * (B // 2))

        @block.gpsimd
        def _(pool):
            pool.memset(ident[:], 0.0).then_inc(consts_zero, 1)
            pool.memset(ones[:], 1.0).then_inc(consts_ready, 1)
            pool.memset(zeros[:], 0.0).then_inc(consts_ready, 1)
            pool.wait_ge(consts_zero, 1)
            pool.affine_select(out=ident[:], in_=ident[:], compare_op=ALU.not_equal, fill=1.0, base=0,
                               pattern=[[-1, P]], channel_multiplier=1).then_inc(consts_ready, 1)
            pool.wait_ge(consts_ready, 3)
            pool.tensor_copy(ident_bf[:], ident[:]).then_inc(consts_ready, 1)
            for tile, value in ((c_eps, EPS), (c_neg, -1.0), (c_half, H_SCALE / 2), (c_three, 1.5 * H_SCALE)):
                pool.memset(tile[:], value).then_inc(consts_ready, 1)
            pool.memset(share[:], 0.0).then_inc(share_zero, 1)
            pool.wait_ge(consts_ready, 8)
            pool.wait_ge(share_zero, 1)

            def normalise(j, k):
                g = j * RING + k
                mean, var = (mean_var[:, k % 2, :, n] for n in range(2))
                scale, shift = (affine[:, k % 2, n] for n in range(2))
                pool.wait_ge(mean_var_ready, (g + 1) * G)
                pool.tensor_tensor(var_eps[:], var, c_eps[:], ALU.add).then_inc(var_eps_ready, 1)
                pool.tensor_tensor(neg_mean[:], mean, c_neg[:], ALU.mult).then_inc(newton_step, 1)
                pool.wait_ge(var_eps_ready, g + 1)
                pool.tensor_tensor(var_half[:], var_eps[:], c_half[:], ALU.mult).then_inc(newton_step, 1)
                pool.wait_ge(inv0_ready, g + 1)
                pool.tensor_tensor(newton_a[:], inv0[:], inv0[:], ALU.mult).then_inc(newton_step, 1)
                pool.wait_ge(newton_step, 6 * g + 3)
                pool.tensor_tensor(newton_b[:], newton_a[:], var_half[:], ALU.mult).then_inc(newton_step, 1)
                pool.wait_ge(newton_step, 6 * g + 4)
                pool.tensor_tensor(newton_c[:], c_three[:], newton_b[:], ALU.subtract).then_inc(newton_step, 1)
                pool.wait_ge(newton_step, 6 * g + 5)
                pool.tensor_tensor(scale, newton_c[:], inv0[:], ALU.mult).then_inc(newton_step, 1)
                pool.wait_ge(newton_step, 6 * g + 6)
                pool.tensor_tensor(shift, neg_mean[:], scale, ALU.mult).then_inc(affine_ready, 1)

            def sum_first(j, k):
                pool.wait_ge(h1_ready, (j * RING + k) * G + 1)
                pool.tensor_tensor(share[:], share[:], x1[:, k, 0], ALU.add).then_inc(share_summed, 1)

            with pool.Fori(0, STEPS - 1) as j:
                for k in range(RING):
                    normalise(j, k)
                    sum_first(j, k)
            for k in range(RING):
                normalise(STEPS - 1, k)
                if k < RING - 2:
                    sum_first(STEPS - 1, k)
            sum_first(STEPS - 1, RING - 2)

            for c in NOISE_POOL:
                make_noise(pool, c, noise_pool)

            def low_first(b):
                pool.wait_ge(h_hi_ready, b + 1)
                low, high = ((first_low0, first_high0), (first_low1, first_high1))[b]
                pool.wait_ge(noise_pool, len(NOISE_POOL))
                pool.tensor_tensor(low[:], first_h[:], high[:], ALU.subtract).then_inc(h_lo_ready, 1)

            low_first(0)
            low_first(1)

            def low_right(i, part):
                high, low, of = right_part(i, part)
                kind, turn = right_turn(i, part)
                pool.wait_ge(right_hi_ready[kind], turn)
                pool.tensor_tensor(low, of, high.bitcast(F32), ALU.subtract).then_inc(right_lo_ready[kind], 1)

            def low_left(p, k):
                pool.wait_ge(left_hi_ready, p * NUM + k + 1)
                pool.tensor_tensor(left[:, k, 1], y[:, LEFT[k]], left[:, k, 0].bitcast(F32),
                                   ALU.subtract).then_inc(left_lo_ready, 1)

            def low_h(b, parity):
                pool.wait_ge(h_hi_ready, b + 1)
                pool.tensor_tensor(h_lo[:, parity], h[:], h_hi[:, parity], ALU.subtract).then_inc(h_lo_ready, 1)

            for s in range(S - 1):
                low_right(s // 2, s % 2)
                if s in (2, 4):
                    low_right(s // 2 - 1, 2)
                    if s == 4:
                        pool.wait_ge(self_ready, S)
                        pool.partition_all_reduce(all_common[:], self_common[:], P, RMAX).then_inc(max_ready, 1)
                    low_right(s // 2 - 1, 3)
            low_left(0, P1)
            low_right(LAST, 1)
            low_left(0, P2)
            low_right(LAST - 1, 2)
            low_left(0, P6)
            low_left(0, P5)
            low_h(2, 0)

            def low_pair(p, first=False, more=True):
                for k in (P7, P3, P4):
                    low_left(p, k)
                if more:
                    if not first:
                        low_h(p * 2 + 2, 0)
                    low_h(p * 2 + 3, 1)
                    for k in (P1, P2, P6, P5):
                        low_left(p + 1, k)

            low_pair(0, first=True)
            with pool.Fori(0, (PAIRS - 2) // 2) as i:
                for k in range(2):
                    low_pair(i * 2 + (k + 1))
            low_pair(PAIRS - 1, more=False)

        @block.scalar
        def _(act):
            act.wait_ge(w_turned, 2)
            act.copy(w_hi[:], ps[:, Y, 0:P]).then_inc(w_hi_ready, 1)

            def stdev_of(g):
                act.wait_ge(var_eps_ready, g + 1)
                act.activation(stdev[:], var_eps[:], ACT.Sqrt).then_inc(stdev_ready, 1)

            def h1(g, k, q):
                act.activation(x1[:, k, q], x1[:, k, q], ACT.Relu, scale=affine[:, k % 2, 0, q:q + 1],
                               bias=affine[:, k % 2, 1, q:q + 1]).then_inc(h1_ready, 1)

            def h1_group(j, k, last=False):
                g = j * RING + k
                act.wait_ge(affine_ready, g + 1)
                for q in range(G):
                    if q == G - 1 and not last:
                        stdev_of(g + 1)
                    h1(g, k, q)

            stdev_of(0)
            with act.Fori(0, STEPS - 1) as j:
                for k in range(RING):
                    h1_group(j, k)
            for k in range(RING):
                h1_group(STEPS - 1, k, last=(k == RING - 1))

            act.wait_ge(total_ready, 1)
            act.activation(avg_sq[:], total[:], ACT.Square, scale=1.0 / (B * H_SCALE)).then_inc(avg_sq_ready, 1)
            act.activation(avg[:], total[:], ACT.Copy, scale=1.0 / (B * H_SCALE)).then_inc(avg_ready, 1)
            act.wait_ge(col_v_ready, 1)
            act.activation(col_sqrt[:], col_v[:], ACT.Sqrt).then_inc(col_sqrt_ready, 1)

            def relu_h(h_, slot, turn):
                scale, shift = (norms[:, ds(turn, 1), n, slot:slot + 1] for n in range(2))
                act.activation(h_[:], x2[slot][:], ACT.Relu, scale=scale, bias=shift).then_inc(h_ready, 1)

            def high_first(b):
                act.wait_ge(x2_in[b], 16)
                if b == 1:
                    act.wait_ge(h_lo_ready, 1)
                act.wait_ge(noise_pool, 1)
                relu_h(first_h, b, 0)
                act.wait_ge(h_ready, b + 1)
                act.wait_ge(noise_pool, len(NOISE_POOL))
                act.copy((first_high0, first_high1)[b][:], first_h[:]).then_inc(h_hi_ready, 1)

            def high_h(b, slot, turn):
                act.wait_ge(x2_in[slot], 16 * (turn + 1))
                act.wait_ge(h_lo_ready, b)
                relu_h(h, slot, turn)
                act.wait_ge(h_ready, b + 1)
                act.wait_ge(y_done, b - 1)
                act.copy(h_hi[:, slot % 2], h[:]).then_inc(h_hi_ready, 1)

            def high_right(i, part):
                high, low, of = right_part(i, part)
                if part < 2:
                    act.wait_ge(weights_ready, 2 * i + part + 1)
                else:
                    act.wait_ge(sums_ready, 4 * i + 2 * part - 2)
                act.copy(high, of).then_inc(right_hi_ready[right_turn(i, part)[0]], 1)

            def high_left(p, k, first=False):
                if k in (P1, P4):
                    act.wait_ge(y_ready, p * 2 + (1 if k == P1 else 2))
                elif k in (P6, P7, P3):
                    act.wait_ge(s_ready, p * 4 + {P6: 2, P7: 3, P3: 4}[k])
                if not first:
                    act.wait_ge(product_done, (p - 1) * NUM + k + 1)
                act.copy(left[:, k, 0], y[:, LEFT[k]]).then_inc(left_hi_ready, 1)

            act.wait_ge(norms_ready, B // G)
            high_first(0)
            high_first(1)
            for s in range(S):
                act.wait_ge(sym_done, s + 1)
                act.copy(adj_t[:, s], ps[:, 2 + s % 2]).then_inc(adj_t_ready, 1)
            for s in range(S):
                act.wait_ge(self_ready, s + 1)
                if s >= 2:
                    act.wait_ge(weights_ready, s - 1)
                    act.wait_ge(degree_ready, s - 1)
                act.activation(square[:, s % 2], ps[:, s % 2], ACT.Square).then_inc(square_all, 1)
                if s == S - 1:
                    act.wait_ge(y_done, 2)
                if s:
                    high_right((s - 1) // 2, (s - 1) % 2)
                if 3 <= s < S - 1 and s % 2:
                    high_right((s - 3) // 2, 2)
                    high_right((s - 3) // 2, 3)
            act.wait_ge(col_v_ready, 2)
            act.activation(col_sqrt[:], col_v[:], ACT.Sqrt).then_inc(col_sqrt_ready, 1)
            high_left(0, P1, first=True)
            high_right(LAST, 1)
            high_left(0, P2, first=True)
            high_right(LAST - 1, 2)
            high_right(LAST - 1, 3)
            high_left(0, P6, first=True)
            act.wait_ge(right_lo_ready[0], 2 * LAST)
            act.wait_ge(sums_ready, 4 * LAST)
            high_right(LAST, 2)
            high_left(0, P5, first=True)
            high_right(LAST, 3)
            high_h(2, 2, 0)

            def high_pair(p, turn, slot, first=False, more=True):
                high_left(p, P7, first)
                act.wait_ge(product_done, p * NUM + P1 + 1)
                if not first:
                    act.wait_ge(c_ready, p * 4 - 1)
                act.copy(u[:, 0], bank(P1)).then_inc(p1_copied, 1)
                high_left(p, P3, first)
                if first:
                    act.wait_ge(row_done, 2)
                    act.wait_ge(sums_ready, 4 * KS)
                    act.wait_ge(right_lo_ready[0], 2 * KS)
                    act.copy(dinv_row[:], ps[:, ROWS]).then_inc(dinv_row_ready, 1)
                high_left(p, P4, first)
                if more:
                    for e in range(1 if first else 0, 2):
                        high_h(p * 2 + (2 + e), slot + e, turn)
                    for k in (P1, P2, P6, P5):
                        high_left(p + 1, k)

            high_pair(0, 0, 2, first=True)
            with act.Fori(1, PAIRS // 2) as i:
                for k in range(2):
                    high_pair(i * 2 + (k - 1), i, 2 * k)
            high_pair(PAIRS - 1, 0, 0, more=False)

        @block.vector
        def _(dve):
            def refine(v, root, inv, tmp, out_, sem_, n0):
                dve.reciprocal(inv, root).then_inc(sem_, 1)
                dve.wait_ge(sem_, n0 + 1)
                dve.tensor_tensor(tmp[0], inv, inv, ALU.mult).then_inc(sem_, 1)
                dve.wait_ge(sem_, n0 + 2)
                dve.tensor_tensor(tmp[1], tmp[0], v, ALU.mult).then_inc(sem_, 1)
                dve.wait_ge(sem_, n0 + 3)
                dve.tensor_scalar(tmp[2], tmp[1], -0.5, 1.5, ALU.mult, ALU.add).then_inc(sem_, 1)
                dve.wait_ge(sem_, n0 + 4)
                dve.tensor_tensor(out_, tmp[2], inv, ALU.mult).then_inc(sem_, 1)
                dve.wait_ge(sem_, n0 + 5)

            dve.wait_ge(w_turned, 1)
            dve.tensor_reduce(w_max[:], ps[:, Y, 0:P], AX_X, ALU.max, apply_absolute_value=True).then_inc(w_pow_step, 1)
            dve.wait_ge(w_pow_step, 1)
            dve.tensor_scalar(w_pow[:], w_max[:], W_MIN, None, ALU.max).then_inc(w_pow_step, 1)
            dve.wait_ge(w_pow_step, 2)
            dve.tensor_scalar(w_pow_inv[:].bitcast(I32), w_pow[:].bitcast(I32), EXPONENT, None,
                              ALU.bitwise_and).then_inc(w_pow_step, 1)
            dve.wait_ge(w_pow_step, 3)
            dve.tensor_scalar(unscale[:], w_pow_inv[:], 1.0 / (W_TOP * H_SCALE), None, ALU.mult).then_inc(w_pow_step, 1)
            dve.reciprocal(w_pow[:], w_pow_inv[:]).then_inc(w_pow_step, 1)
            dve.wait_ge(w_pow_step, 5)
            dve.tensor_scalar(w_cols[:], ps[:, Y, 0:P], w_pow[:, 0:1], W_TOP, ALU.mult, ALU.mult).then_inc(w_cols_ready, 1)
            dve.wait_ge(w_hi_ready, 1)
            dve.tensor_tensor(w_lo[:], ps[:, Y, 0:P], w_hi[:], ALU.subtract).then_inc(w_lo_ready, 1)

            def invert(g):
                dve.wait_ge(stdev_ready, g + 1)
                dve.reciprocal(inv0[:], stdev[:]).then_inc(inv0_ready, 1)

            def note(g, parity):
                dve.wait_ge(affine_ready, g + 1)
                dve.tensor_scalar(norms[:, ds(g, 1)], affine[:, parity:parity + 1], 1.0, None,
                                  ALU.mult).then_inc(norms_ready, 1)

            def statistics(j, k, first=False):
                g = j * RING + k
                for q in range(G):
                    if q % 2 == 0:
                        dve.wait_ge(x1_in[k][q // 2], 16 * (j + 1))
                    dve.bn_stats(halves[:, k % 2, q, 0], x1[:, k, q, 0:H]).then_inc(halves_ready, 1)
                    if q:
                        dve.wait_ge(halves_ready, (g * G + q) * 2)
                    dve.bn_stats(halves[:, k % 2, q, 1], x1[:, k, q, H:N]).then_inc(halves_ready, 1)
                    if q:
                        dve.bn_aggr(mean_var[:, k % 2, q - 1], halves[:, k % 2, q - 1]).then_inc(mean_var_ready, 1)
                    if q == 0 and not first:
                        invert(g - 1)
                    if q == G - 1 and not first:
                        note(g - 1, (k - 1) % 2)
                dve.wait_ge(halves_ready, (g + 1) * G * 2)
                dve.memset(waiting[:], 0.0)
                dve.bn_aggr(mean_var[:, k % 2, G - 1], halves[:, k % 2, G - 1]).then_inc(mean_var_ready, 1)

            for k in range(RING):
                statistics(0, k, first=(k == 0))
            with dve.Fori(1, STEPS) as j:
                for k in range(RING):
                    statistics(j, k)
            invert(B // G - 1)
            note(B // G - 1, 1)
            for n, q in enumerate((0, 3)):
                dve.wait_ge(h1_ready, B - G + q + 1)
                dve.wait_ge(share_summed, B // G - 1 + n)
                dve.tensor_tensor(share[:], share[:], x1[:, RING - 1, q], ALU.add).then_inc(share_summed, 1)
            dve.wait_ge(share_summed, B // G + 1)
            dve.wait_ge(sum_done, 1)
            dve.tensor_tensor(total[:], ps[:, SUM], share[:], ALU.add).then_inc(total_ready, 1)

            make_noise(dve, 1, noise_dve)
            make_noise(dve, 3, noise_dve)
            dve.wait_ge(sumsq_done, 1)
            dve.tensor_scalar(col_v[:], ps[:, COLS, 0:S], NORM_MIN ** 2, None, ALU.max).then_inc(col_v_ready, 1)
            dve.wait_ge(col_sqrt_ready, 1)
            cols = (col_a[:], col_b[:], col_c[:])
            refine(col_v[:], col_sqrt[:], col_inv[:], cols, inv_norm[:], col_step, 0)
            dve.tensor_copy(wide[0][:], inv_norm[:].unsqueeze(2).to_broadcast([P, S, P])).then_inc(wide_ready, 1)
            make_noise(dve, 5, noise_dve)
            dve.wait_ge(row_done, 1)
            dve.wait_ge(avg_ready, 1)
            dve.tensor_tensor(feats_hi[:], avg[:], ps[:, ROWS], ALU.mult).then_inc(feats_ready, 1)
            dve.tensor_tensor(feats[:], avg[:], ps[:, ROWS], ALU.mult).then_inc(feats_ready, 1)
            dve.wait_ge(feats_ready, 2)
            dve.tensor_tensor(feats_lo[:], feats[:], feats_hi[:].bitcast(F32), ALU.subtract).then_inc(feats_ready, 1)

            for s in range(S):
                for noises, ready in ((NOISE_POOL, noise_pool), (NOISE_DVE, noise_dve)):
                    if s in noises:
                        dve.wait_ge(ready, noises.index(s) + 1)
                dve.wait_ge(sim_done, s + 1)
                dve.tensor_tensor(adj[:, s], ps[:, s % 4], noise[:, s], ALU.is_gt).then_inc(adj_ready, 1)
            for s in range(S):
                node = slice(s * P, s * P + P)
                dve.wait_ge(adj_t_ready, s + 1)
                dve.tensor_tensor(nmask[:, s], adj[:, s], adj_t[:, s], ALU.max).then_inc(nmask_offdiag, 1)
                dve.wait_ge(nmask_offdiag, s + 1)
                dve.tensor_tensor(nmask[:, s, node], nmask[:, s, node], ident_bf[:], ALU.max).then_inc(nmask_ready, 1)
            def self_count(s):
                dve.wait_ge(common_done, s + 1)
                dve.tensor_reduce(self_common[:, s:s + 1], ps[:, s % 2, s * P:s * P + P], AX_X,
                                  ALU.max).then_inc(self_ready, 1)

            def drop_single(s):
                node = slice(s * P, s * P + P)
                dve.wait_ge(square_all, s + 1)
                dve.scalar_tensor_tensor(out=square[:, s % 2, node], in0=square[:, s % 2, node], scalar=1.0,
                                         in1=square[:, s % 2, node], op0=ALU.is_gt,
                                         op1=ALU.mult).then_inc(square_ready, 1)

            def sum_degree(s):
                dve.wait_ge(square_ready, s + 1)
                dve.tensor_tensor_reduce(products[:], square[:, s % 2], adj_t[:, s], 1.0, 0.0, ALU.mult, ALU.add,
                                         degree[:, place_of(s):place_of(s) + 1]).then_inc(degree_ready, 1)

            def weigh(s):
                if s >= 4:
                    dve.wait_ge(right_lo_ready[0], s // 2 * 2 - 2)
                dve.tensor_tensor(edges[s // 2 % 2][:, s % 2], rows_of_half(square[:, s % 2]), rows_of_half(adj[:, s]),
                                  ALU.mult).then_inc(weights_ready, 1)

            def sum_blocks(i, part):
                b11, b12, b21, b22 = (edges[i % 2][:, n, m] for n in range(2) for m in range(2))
                t3, t2, t1, t4 = (sums[i % 2][:, n] for n in range(4))
                if part == 0:
                    dve.wait_ge(weights_ready, 2 * i + 2)
                    if i >= 2:
                        dve.wait_ge(right_lo_ready[1], 2 * i - 2)
                    dve.tensor_tensor(t3, b22, b12, ALU.subtract).then_inc(sums_ready, 1)
                    dve.wait_ge(sums_ready, 4 * i + 1)
                    dve.tensor_tensor(t2, t3, b11, ALU.add).then_inc(sums_ready, 1)
                else:
                    dve.tensor_tensor(t1, b12, b11, ALU.subtract).then_inc(sums_ready, 1)
                    dve.wait_ge(sums_ready, 4 * i + 2)
                    dve.tensor_tensor(t4, b21, t2, ALU.subtract).then_inc(sums_ready, 1)

            for s in range(S):
                if 0 < s < S - 1:
                    sum_degree(s - 1)
                self_count(s)
                if 0 < s < S - 1:
                    weigh(s - 1)
                elif s:
                    sum_degree(s - 1)
                drop_single(s)
                if 0 < s < S - 2 and s % 2 == 0:
                    sum_blocks(s // 2 - 1, 0)
                    sum_blocks(s // 2 - 1, 1)
            sum_degree(S - 1)
            weigh(S - 2)

            dve.wait_ge(max_ready, 1)
            dve.tensor_reduce(max_common[:], all_common[:], AX_X, ALU.max).then_inc(col_step, 1)
            dve.wait_ge(col_step, 6)
            dve.reciprocal(inv_max[:], max_common[:]).then_inc(col_step, 1)
            dve.wait_ge(col_step, 7)
            dve.wait_ge(degree_ready, S)
            dve.tensor_scalar(degree_n[:], degree[:], inv_max[:, 0:1], None, ALU.mult).then_inc(col_step, 1)
            dve.wait_ge(col_step, 8)
            dve.tensor_scalar(col_v[:], degree_n[:], DEG_MIN, None, ALU.max).then_inc(col_v_ready, 1)
            dve.tensor_scalar(has_edge[:], degree_n[:], 0.0, None, ALU.is_gt).then_inc(col_step, 1)
            dve.wait_ge(col_sqrt_ready, 2)
            refine(col_v[:], col_sqrt[:], col_inv[:], cols, inv_norm[:], col_step, 9)
            dve.tensor_tensor(dinv[:], inv_norm[:], has_edge[:], ALU.mult).then_inc(dinv_ready, 1)
            dve.wait_ge(dinv_ready, 1)
            dinv_rows = dinv[:].unsqueeze(2).to_broadcast([P, S, P])

            def scale_y(b, e, splits):
                dve.wait_ge(y_done, b + 1)
                if splits is not None:
                    dve.wait_ge(left_lo_ready, splits)
                dve.tensor_tensor(y[:, 2 * e:2 * e + 2].rearrange("p e (c n) -> p (e c) n", n=P), rows(y_bank(e)),
                                  dinv_rows, ALU.mult).then_inc(y_ready, 1)

            def sum_rows(p, n):
                if n == 1:
                    dve.wait_ge(y_ready, p * 2 + 2)
                    dve.tensor_tensor(y[:, S1], y[:, A21], y[:, A22], ALU.add).then_inc(s_ready, 1)
                elif n == 2:
                    dve.wait_ge(s_ready, p * 4 + 1)
                    dve.tensor_tensor(y[:, S2], y[:, S1], y[:, A11], ALU.subtract).then_inc(s_ready, 1)
                elif n == 3:
                    dve.wait_ge(s_ready, p * 4 + 2)
                    dve.tensor_tensor(y[:, A21], y[:, A11], y[:, A21], ALU.subtract).then_inc(s_ready, 1)
                else:
                    dve.wait_ge(s_ready, p * 4 + 3)
                    dve.wait_ge(left_lo_ready, p * NUM + P2 + 1)
                    dve.tensor_tensor(y[:, A12], y[:, A12], y[:, S2], ALU.subtract).then_inc(s_ready, 1)

            def add_u2(p):
                dve.wait_ge(product_done, p * NUM + P6 + 1)
                dve.tensor_tensor(u[:, 1], u[:, 0], bank(P6), ALU.add).then_inc(u2_ready, 1)

            def add_u4(p):
                dve.wait_ge(u2_ready, p + 1)
                dve.wait_ge(product_done, p * NUM + P5 + 1)
                dve.tensor_tensor(u[:, 0], u[:, 1], bank(P5), ALU.add).then_inc(u4_ready, 1)

            def add_u3(p):
                dve.tensor_tensor(u[:, 1], u[:, 1], bank(P7), ALU.add).then_inc(u3_ready, 1)

            def half(e, m):
                return result[:, e, m * H:m * H + H]

            def add_bias_x(e, m, slot):
                dve.scalar_tensor_tensor(out=half(e, m), in0=half(e, m), scalar=bias_sb[:, 0:1],
                                         in1=x2[slot][:, m * H:m * H + H], op0=ALU.add,
                                         op1=ALU.add).then_inc(result_ready[e], 1)

            def add_c(p, n, k, e, m, addend):
                dve.wait_ge(product_done, p * NUM + k + 1)
                dve.tensor_tensor(half(e, m), addend, bank(k), ALU.add).then_inc(c_ready, 1)

            def finish_c(p, n, e, m, slot):
                dve.wait_ge(c_ready, p * 4 + n)
                dve.scalar_tensor_tensor(out=half(e, m), in0=half(e, m), scalar=unscale[:, 0:1],
                                         in1=dinv_row[:, m * H:m * H + H], op0=ALU.mult,
                                         op1=ALU.mult).then_inc(scaled_ready, 1)
                dve.wait_ge(scaled_ready, p * 4 + n)
                add_bias_x(e, m, slot)

            def split(i, part, ready):
                high, low, of = right_part(i, part)
                dve.wait_ge(right_hi_ready[1], 2 * i + part - 1)
                dve.tensor_tensor(low, of, high.bitcast(F32), ALU.subtract).then_inc(ready, 1)

            def split_last(part):
                dve.wait_ge(right_lo_ready[1], 2 * LAST + part - 3)
                split(LAST, part, right_lo_last)

            scale_y(0, 0, None)
            dve.tensor_scalar(dinv_out[:], dinv[:], inv_max[:, 0:1], None, ALU.mult).then_inc(dinv_ready, 1)
            weigh(S - 1)
            scale_y(1, 1, None)
            sum_blocks(LAST - 1, 0)
            sum_blocks(LAST - 1, 1)
            sum_rows(0, 1)
            sum_rows(0, 2)
            sum_blocks(LAST, 0)
            sum_blocks(LAST, 1)
            split_last(2)
            split(LAST - 1, 3, right_lo_ready[1])
            split_last(3)
            dve.wait_ge(dinv_ready, 2)
            dve.tensor_copy(wide[1][:], dinv_out[:].unsqueeze(2).to_broadcast([P, S, P])).then_inc(wide_ready, 1)
            sum_rows(0, 3)
            sum_rows(0, 4)

            def pair(p, slot, first=False, more=True):
                if first:
                    dve.wait_ge(right_lo_last, 2)
                else:
                    dve.wait_ge(result_stored[0], p * 16)
                dve.wait_ge(p1_copied, p + 1)
                add_c(p, 1, P2, 0, 0, u[:, 0])
                add_u2(p)
                if first:
                    dve.wait_ge(dinv_row_ready, 1)
                finish_c(p, 1, 0, 0, slot)
                add_u4(p)
                if more:
                    scale_y(p * 2 + 2, 0, p * NUM + NUM - 1)
                if not first:
                    dve.wait_ge(result_stored[1], p * 16)
                dve.wait_ge(u4_ready, p + 1)
                add_c(p, 2, P7, 1, 1, u[:, 0])
                add_u3(p)
                finish_c(p, 2, 1, 1, slot + 1)
                add_c(p, 3, P3, 0, 1, u[:, 0])
                finish_c(p, 3, 0, 1, slot)
                if more:
                    scale_y(p * 2 + 3, 1, p * NUM + NUM)
                    sum_rows(p + 1, 1)
                    sum_rows(p + 1, 2)
                dve.wait_ge(u3_ready, p + 1)
                add_c(p, 4, P4, 1, 0, u[:, 1])
                finish_c(p, 4, 1, 0, slot + 1)
                if more:
                    sum_rows(p + 1, 3)
                    sum_rows(p + 1, 4)

            pair(0, 0, first=True)
            with dve.Fori(0, (PAIRS - 2) // 2) as i:
                for k in range(2):
                    pair(i * 2 + (k + 1), (2 * k + 2) % XB)
            pair(PAIRS - 1, 2, more=False)

        @block.tensor
        def _(pe):
            def turn(src):
                pe.transpose(ps[:, Y, 0:P], src, ident[:]).then_inc(w_turned, 1)

            pe.wait_ge(consts_ready, 4)
            for half in range(2):
                pe.matmul(ps[:, SUM, half * H:half * H + H], ident[:], zeros[:], start=True, stop=False)
            pe.wait_ge(params_in, 32)
            turn(w_in[:])
            pe.wait_ge(w_cols_ready, 1)
            turn(w_cols[:])
            def sum_rest(j, k, elements=range(1, G), last=False):
                for q in elements:
                    pe.wait_ge(h1_ready, (j * RING + k) * G + q + 1)
                    for half in range(2):
                        mm = pe.matmul(ps[:, SUM, half * H:half * H + H], ident[:],
                                       x1[:, k, q, half * H:half * H + H], start=False, stop=(last and q == elements[-1]))
                    if not last and q % 2:
                        mm.then_inc(pair_summed[q // 2], 1)
                if last:
                    mm.then_inc(sum_done, 1)

            with pe.Fori(0, STEPS - 1) as j:
                for k in range(RING):
                    sum_rest(j, k)
            for k in range(RING - 1):
                sum_rest(STEPS - 1, k)
            sum_rest(STEPS - 1, RING - 1, (1, 2), last=True)

            pe.wait_ge(avg_sq_ready, 1)
            for s in range(S):
                mm = pe.matmul(ps[:, COLS, s:s + 1], avg_sq[:, s * P:s * P + P], ones[:, 0:1], start=True, stop=True)
            mm.then_inc(sumsq_done, 1)

            def spread(n, order):
                pe.wait_ge(wide_ready, n + 1)
                for s in range(S):
                    mm = pe.matmul(ps[:, ROWS, s * P:s * P + P], wide[n][:, order(s)], ident[:], start=True, stop=True)
                mm.then_inc(row_done, 1)

            spread(0, lambda s: s)
            def similar(s, left_, right_, opens=False, closes=False):
                for half in range(2):
                    mm = pe.matmul(ps[:, s % 4, half * H:half * H + H], left_[:, s * P:s * P + P],
                                   right_[:, half * H:half * H + H], start=opens, stop=closes)
                return mm

            pe.wait_ge(feats_ready, 1)
            for s in range(4):
                if s == ROWS:
                    pe.wait_ge(feats_ready, 2)
                similar(s, feats_hi, feats_hi, opens=True)
            pe.wait_ge(feats_ready, 3)
            for s in range(S):
                if s >= 4:
                    pe.wait_ge(adj_ready, s - 3)
                    similar(s, feats_hi, feats_hi, opens=True)
                similar(s, feats_hi, feats_lo)
                similar(s, feats_lo, feats_hi, closes=True).then_inc(sim_done, 1)
            def transpose_edges(s):
                if s >= 2:
                    pe.wait_ge(adj_t_ready, s - 1)
                for d in range(S):
                    mm = pe.matmul(ps[:, 2 + s % 2, d * P:d * P + P], adj[:, d, s * P:s * P + P], ident_bf[:],
                                   start=True, stop=True)
                mm.then_inc(sym_done, 1)

            def common_step(s, c):
                for half in range(2):
                    mm = pe.matmul(ps[:, s % 2, half * H:half * H + H], nmask[:, c, s * P:s * P + P],
                                   nmask[:, c, half * H:half * H + H], start=(c == 0), stop=(c == S - 1))
                if c == S - 1:
                    mm.then_inc(common_done, 1)

            pe.wait_ge(adj_ready, S)
            transpose_edges(0)
            transpose_edges(1)
            for c in range(S):
                if c + 2 < S:
                    transpose_edges(c + 2)
                pe.wait_ge(nmask_ready, c + 1)
                common_step(0, c)
                common_step(1, c)

            for s in range(2, S):
                pe.wait_ge(square_all, s - 1)
                for c in range(S):
                    common_step(s, c)

            def project(b, e, high, low):
                pe.wait_ge(h_hi_ready, b + 1)
                pe.wait_ge(h_lo_ready, b + 1)
                for s in range(S):
                    node = slice(s * P, s * P + P)
                    out_ = y_bank(e)[:, place_of(s) * P:place_of(s) * P + P]
                    pe.matmul(out_, high[:, node], w_hi[:], start=True, stop=False)
                    pe.matmul(out_, high[:, node], w_lo[:], start=False, stop=False)
                    mm = pe.matmul(out_, low[:, node], w_hi[:], start=False, stop=True)
                mm.then_inc(y_done, 1)

            def product(p, k, first=False):
                right = RIGHT[k]
                part = (0, 1, 1, 2, 2, 3, 3)[right]
                kind = part // 2
                pe.wait_ge(left_hi_ready, p * NUM + k + 1)
                for i in range(KS):
                    for right_ready, half_ in ((right_hi_ready, right_hi), (right_lo_ready, right_lo)):
                        if first and i == LAST and kind == 1 and half_ is right_lo:
                            pe.wait_ge(right_lo_last, part - 1)
                        elif first:
                            pe.wait_ge(right_ready[kind], right_turn(i, part)[1])
                        pe.matmul(bank(k), left[:, k, 0, i * P:i * P + P], half_[:, i, right],
                                  start=(i == 0 and half_ is right_hi), stop=False)
                pe.wait_ge(left_lo_ready, p * NUM + k + 1)
                for i in range(KS):
                    mm = pe.matmul(bank(k), left[:, k, 1, i * P:i * P + P], right_hi[:, i, right],
                                   start=False, stop=(i == KS - 1))
                mm.then_inc(product_done, 1)

            def pair(p, first=False, more=True):
                if not first:
                    pe.wait_ge(u3_ready, p)
                product(p, P1, first)
                if not first:
                    pe.wait_ge(c_ready, p * 4 - 1)
                product(p, P2, first)
                if not first:
                    pe.wait_ge(c_ready, p * 4)
                product(p, P6, first)
                if not first:
                    pe.wait_ge(u4_ready, p)
                product(p, P5, first)
                if first:
                    spread(1, place_of)
                pe.wait_ge(p1_copied, p + 1)
                product(p, P7, first)
                if more:
                    if first:
                        pe.wait_ge(dinv_row_ready, 1)
                    else:
                        pe.wait_ge(y_ready, p * 2 + 2)
                    project(p * 2 + 2, 0, h_hi[:, 0], h_lo[:, 0])
                pe.wait_ge(c_ready, p * 4 + 1)
                product(p, P3, first)
                if more:
                    project(p * 2 + 3, 1, h_hi[:, 1], h_lo[:, 1])
                pe.wait_ge(u2_ready, p + 1)
                product(p, P4, first)

            pe.wait_ge(w_lo_ready, 1)
            pe.wait_ge(adj_t_ready, S)
            project(0, 0, first_high0, first_low0)
            project(1, 1, first_high1, first_low1)
            pe.wait_ge(square_all, S)
            pe.wait_ge(self_ready, S)
            pair(0, first=True)
            with pe.Fori(0, (PAIRS - 2) // 2) as i:
                for k in range(2):
                    pair(i * 2 + (k + 1))
            pair(PAIRS - 1, more=False)


_INS = ['x', 'adj', 'L0_gnn_bias', 'L0_gnn_gumbel']
_OUTS = [((64, 128, 1024), 'float32')]


def kernel(**inputs):
    import numpy as _np
    import concourse.bacc as _bacc
    from concourse import mybir as _mybir
    from concourse.bass_utils import run_bass_kernel_spmd as _run

    nc = _bacc.Bacc("TRN2", target_bir_lowering=False, num_devices=1)
    arrays, args = {}, []
    for name in _INS:
        a = _np.ascontiguousarray(inputs[name])
        arrays[f"in_{name}_dram"] = a
        args.append(nc.dram_tensor(f"in_{name}_dram", a.shape, _mybir.dt.from_np(a.dtype), kind="ExternalInput").ap())
    for i, (shape, dtype) in enumerate(_OUTS):
        dt = _mybir.dt.from_np(_np.dtype(dtype))
        args.append(nc.dram_tensor(f"out_{i}_dram", shape, dt, kind="ExternalOutput").ap())
    gnn_program(nc, *args)
    r = _run(nc, [arrays], core_ids=[0])
    got = tuple(r.results[0][f"out_{i}_dram"] for i in range(len(_OUTS)))
    return got[0]
```
